# Optimizing a Trainium2 kernel written in Bass

```python
import numpy as np
import jax
import jax.numpy as jnp

def _softmax(x, axis=-1):
    return jax.nn.softmax(x, axis=axis)

def _gelu(x):
    return jax.nn.gelu(x, approximate=True)

def _silu(x):
    return jax.nn.silu(x)

def _sigmoid(x):
    return jax.nn.sigmoid(x)

def _layernorm(x, axis=-1, eps=1e-05):
    m = jnp.mean(x, axis=axis, keepdims=True)
    v = jnp.var(x, axis=axis, keepdims=True)
    return (x - m) / jnp.sqrt(v + eps)

def _scatter_add(tgt, idx, src, axis=0):
    return tgt.at[idx].add(src)

def _segment_sum(src, seg, n):
    return jax.ops.segment_sum(src, seg, n)
kernel_name = 'mk_xattn_seq_d1_seqx_r4_fb2be4'

def setup_inputs(seed: int=0):
    np.random.seed(seed)
    _w = jnp.asarray

    def _rec_inputs():
        import jax
        import jax.numpy as jnp
        _rk = jax.random.key(seed)
        x = -0.0001233 + 1 * jax.random.normal(jax.random.fold_in(_rk, 1), (64, 256, 320), jnp.float32)
        _lenS = 256 - jax.random.randint(jax.random.fold_in(_rk, 7), (64,), 0, max(1, 256 // 4) + 1, jnp.int32)
        _lenS2 = 120 - jax.random.randint(jax.random.fold_in(_rk, 8), (64,), 0, max(1, 120 // 4) + 1, jnp.int32)
        _ctx_2048P = jax.random.normal(jax.random.fold_in(_rk, 11), (64, 16, 512), jnp.float32)
        _ctx_2048c = jax.random.dirichlet(jax.random.fold_in(_rk, 511), 0.3 * jnp.ones((16,), jnp.float32), (64, 120))
        _ctx_2048t = jnp.einsum('bsk,bkd->bsd', _ctx_2048c, _ctx_2048P)
        _ctx_2048t = _ctx_2048t * jax.lax.rsqrt(jnp.mean(jnp.square(_ctx_2048t)) + 1e-12) * 0.953939
        ctx_2048 = 0.00266749 + 0.998873 * (_ctx_2048t + 0.3 * jax.random.normal(jax.random.fold_in(_rk, 611), (64, 120, 512), jnp.float32))
        return (x, ctx_2048)
    x, ctx_2048 = _rec_inputs()

    def _L0_xattn_setup():
        import jax, jax.numpy as jnp
        import numpy as np
        B, S, C = (2, 1024, 320)
        CA = 512
        HEADS = 20
        HD = C // HEADS
        N_TXT, N_OBJ, N_OTH, N_IP = (77, 4, 4, 16)
        SCALE_OBJ = SCALE_OTH = SCALE_IP = 1.0
        RESCALE = 1.0

        def _heads(x):
            b, l, _ = x.shape
            return x.reshape(b, l, HEADS, HD).transpose(0, 2, 1, 3)

        def _merge(x):
            b, h, l, d = x.shape
            return x.transpose(0, 2, 1, 3).reshape(b, l, h * d)

        def _sdpa(q, k, v):
            scale = 1.0 / np.sqrt(HD).astype(np.float32)
            s = jnp.einsum('bhqd,bhkd->bhqk', q, k) * scale
            p = jax.nn.softmax(s, axis=-1)
            return jnp.einsum('bhqk,bhkd->bhqd', p, v)
        key = jax.random.key(seed)
        ks = jax.random.split(key, 16)
        g = lambda k, shp, fan: jax.random.normal(k, shp, jnp.float32) / np.sqrt(fan).astype(np.float32)
        return {'hidden_states': jax.random.normal(ks[0], (B, S, C), jnp.float32), 'encoder_hidden_states': jax.random.normal(ks[1], (B, N_TXT + N_OBJ + N_OTH + N_IP, CA), jnp.float32), 'to_q_w': g(ks[2], (C, C), C), 'to_k_w': g(ks[3], (CA, C), CA), 'to_v_w': g(ks[4], (CA, C), CA), 'to_k_object_w': g(ks[5], (CA, C), CA), 'to_v_object_w': g(ks[6], (CA, C), CA), 'to_k_others_w': g(ks[7], (CA, C), CA), 'to_v_others_w': g(ks[8], (CA, C), CA), 'to_k_ip_w': g(ks[9], (CA, C), CA), 'to_v_ip_w': g(ks[10], (CA, C), CA), 'to_out_w': g(ks[11], (C, C), C), 'to_out_b': jnp.zeros((C,), jnp.float32)}
    _L0_xattn_all = _L0_xattn_setup()
    _L0_xattn_in = {k: v for k, v in _L0_xattn_all.items() if k in ('to_q_w', 'to_k_w', 'to_v_w', 'to_k_object_w', 'to_v_object_w', 'to_k_others_w', 'to_v_others_w', 'to_k_ip_w', 'to_v_ip_w', 'to_out_w', 'to_out_b')}
    del _L0_xattn_all
    return {'x': x, 'ctx_2048': ctx_2048, 'L0_xattn_to_q_w': _L0_xattn_in['to_q_w'], 'L0_xattn_to_k_w': _L0_xattn_in['to_k_w'], 'L0_xattn_to_v_w': _L0_xattn_in['to_v_w'], 'L0_xattn_to_k_object_w': _L0_xattn_in['to_k_object_w'], 'L0_xattn_to_v_object_w': _L0_xattn_in['to_v_object_w'], 'L0_xattn_to_k_others_w': _L0_xattn_in['to_k_others_w'], 'L0_xattn_to_v_others_w': _L0_xattn_in['to_v_others_w'], 'L0_xattn_to_k_ip_w': _L0_xattn_in['to_k_ip_w'], 'L0_xattn_to_v_ip_w': _L0_xattn_in['to_v_ip_w'], 'L0_xattn_to_out_w': _L0_xattn_in['to_out_w'], 'L0_xattn_to_out_b': _L0_xattn_in['to_out_b']}

def reference(x, ctx_2048, L0_xattn_to_q_w, L0_xattn_to_k_w, L0_xattn_to_v_w, L0_xattn_to_k_object_w, L0_xattn_to_v_object_w, L0_xattn_to_k_others_w, L0_xattn_to_v_others_w, L0_xattn_to_k_ip_w, L0_xattn_to_v_ip_w, L0_xattn_to_out_w, L0_xattn_to_out_b):
    import jax
    import jax.numpy as jnp

    def _L0_xattn_ref(hidden_states, encoder_hidden_states, to_q_w, to_k_w, to_v_w, to_k_object_w, to_v_object_w, to_k_others_w, to_v_others_w, to_k_ip_w, to_v_ip_w, to_out_w, to_out_b):
        import jax, jax.numpy as jnp
        import numpy as np
        B, S, C = (2, 1024, 320)
        CA = 512
        HEADS = 20
        HD = C // HEADS
        N_TXT, N_OBJ, N_OTH, N_IP = (77, 4, 4, 16)
        SCALE_OBJ = SCALE_OTH = SCALE_IP = 1.0
        RESCALE = 1.0

        def _heads(x):
            b, l, _ = x.shape
            return x.reshape(b, l, HEADS, HD).transpose(0, 2, 1, 3)

        def _merge(x):
            b, h, l, d = x.shape
            return x.transpose(0, 2, 1, 3).reshape(b, l, h * d)

        def _sdpa(q, k, v):
            scale = 1.0 / np.sqrt(HD).astype(np.float32)
            s = jnp.einsum('bhqd,bhkd->bhqk', q, k) * scale
            p = jax.nn.softmax(s, axis=-1)
            return jnp.einsum('bhqk,bhkd->bhqd', p, v)
        residual = hidden_states
        end = N_TXT
        ehs_txt = encoder_hidden_states[:, :end]
        ehs_obj = encoder_hidden_states[:, end:end + N_OBJ]
        ehs_oth = encoder_hidden_states[:, end + N_OBJ:end + N_OBJ + N_OTH]
        ehs_ip = encoder_hidden_states[:, end + N_OBJ + N_OTH:]
        q = _heads(hidden_states @ to_q_w)
        h_txt = _sdpa(q, _heads(ehs_txt @ to_k_w), _heads(ehs_txt @ to_v_w))
        h_obj = _sdpa(q, _heads(ehs_obj @ to_k_object_w), _heads(ehs_obj @ to_v_object_w))
        h_oth = _sdpa(q, _heads(ehs_oth @ to_k_others_w), _heads(ehs_oth @ to_v_others_w))
        h_ip = _sdpa(q, _heads(ehs_ip @ to_k_ip_w), _heads(ehs_ip @ to_v_ip_w))
        out = _merge(h_txt) + SCALE_OBJ * _merge(h_obj) + SCALE_OTH * _merge(h_oth) + SCALE_IP * _merge(h_ip)
        out = out @ to_out_w + to_out_b
        out = (out + residual) / RESCALE
        return out
    x = _L0_xattn_ref(x, ctx_2048, L0_xattn_to_q_w, L0_xattn_to_k_w, L0_xattn_to_v_w, L0_xattn_to_k_object_w, L0_xattn_to_v_object_w, L0_xattn_to_k_others_w, L0_xattn_to_v_others_w, L0_xattn_to_k_ip_w, L0_xattn_to_v_ip_w, L0_xattn_to_out_w, L0_xattn_to_out_b)
    return x

_drawn_inputs = setup_inputs


def setup_inputs(seed=0):
    import zlib

    import numpy as np

    out = dict(_drawn_inputs(seed))
    spreads = {'L0_xattn_to_out_b': (0.0, 0.1)}
    factors = {}
    for name, (base, spread) in spreads.items():
        noise = np.random.default_rng([zlib.crc32(name.encode()), seed]).standard_normal(out[name].shape)
        drawn = base * np.exp(spread * noise) if base else spread * noise
        out[name] = jnp.asarray(drawn.astype(out[name].dtype))
    for name, factor in factors.items():
        out[name] = (out[name] * factor).astype(out[name].dtype)
    return out
```

```python
import concourse.bass as bass
from concourse import mybir
from contextlib import ExitStack

F32 = mybir.dt.float32
BF16 = mybir.dt.bfloat16
ALU = mybir.AluOpType
ACT = mybir.ActivationFunctionType
AX = mybir.AxisListType

B, S, C = 64, 256, 320
CTX, NKEY = 512, 120
HEADS, HD = 20, 16
SEG = [(0, 77), (77, 4), (81, 4), (85, 35)]
NSEG = len(SEG)
SCALE = HD ** -0.5

P = 128
G = 5
NC = 3
SLOTS = 8 * NC
PARTS = 3
QPART = [0, 0, 0, 1, 1, 2]
NROW = HD * len(QPART)
SHIFT = PARTS * NSEG
UNITS = 10

KC = CTX // P
PB = 8
NBLOCK = B // PB
TXT, IPS = PB * SEG[0][1], PB * SEG[3][1]
TOK = TXT + IPS
SMALL = B * SEG[1][1]
KTILES = [(0, 4, 0, 0), (4, 4, TXT // 2, 0), (0, 8, TXT, 3)]


def tiles_of(first, count):
    return [(first + at, min(P, count - at), at) for at in range(0, count, P)]


VTILES = [(0, *t) for t in tiles_of(0, TXT)] + [(3, *t) for t in tiles_of(TXT, IPS)]
NV = 4
KB = 3


def slot(n):
    g, j = divmod(n, 4)
    return 3 * (4 * (g % 2) + j) + g // 2


def context_phase(nc, ctx_main, ctx_small, wk, wv, k_parts, v_rows):
    ctx = ExitStack()
    with ctx:
        def sb(name, shape, dt):
            return ctx.enter_context(nc.sbuf_tensor(name, shape, dt))

        def sem(name):
            return ctx.enter_context(nc.semaphore(name))

        wk_sb = sb("wk_sb", [P, NSEG, KC, NC * P], F32)
        wv_sb = sb("wv_sb", [P, NSEG, KC, C], F32)
        small = sb("small", [P, KC, 2 * SMALL], F32)
        tok = sb("tok", [P, 2, KC, TOK], F32)
        k_small = sb("k_small", [P, PARTS, NC, B, 8], BF16)
        k_blk = sb("k_blk", [P, 2, PARTS, PB, NC, NKEY], BF16)
        rest = sb("rest", [P, 2, 512], F32)
        v_pad = sb("v_pad", [P, NV, G, 4, 32], F32)
        k_ps = [ctx.enter_context(nc.psum_tensor(f"k_ps{i}", [P, 512], F32)) for i in range(KB)]
        v_ps = [ctx.enter_context(nc.psum_tensor(f"v_ps{i}", [P, 512], F32)) for i in range(4)]

        w_in = [sem(f"w_in{s}") for s in range(NSEG)]
        small_in = sem("small_in")
        tok_in = [sem("tok_in0"), sem("tok_in1")]
        k_out = [sem("k_out0"), sem("k_out1")]
        v_out = [sem(f"v_out{i}") for i in range(NV)]
        k_proj = sem("k_proj")
        k_hi = sem("k_hi")
        k_rest = sem("k_rest")
        k_mid = sem("k_mid")
        k_lo = sem("k_lo")
        k_fill = sem("k_fill")
        v_proj = sem("v_proj")
        v_cast = sem("v_cast")
        v_zero = sem("v_zero")

        NKT, NVT = len(KTILES) * NC, len(VTILES)
        SKT, SVT = 2 * NC, 4

        block = ctx.enter_context(nc.Block())

        @block.sync
        def _(sp):
            for s in (1, 2, 0, 3):
                sp.dma_start(wk_sb[:, s, :, :], wk[s].rearrange("(k p) n -> p k n", p=P)).then_inc(w_in[s], 16)
                if s == 1:
                    sp.dma_start(small[:, :, :], ctx_small.rearrange("(k p) n -> p k n", p=P)).then_inc(small_in, 16)
                sp.dma_start(wv_sb[:, s, :, :], wv[s].rearrange("(k p) n -> p k n", p=P)).then_inc(w_in[s], 16)

            def load_block(k, r):
                sp.dma_start(tok[:, r, :, :],
                             ctx_main[bass.ds(k, 1), :, :].rearrange("o (k p) n -> p (o k) n", p=P)).then_inc(tok_in[r], 16)

            def store_block(k, r):
                sp.wait_ge(k_lo, SKT + NKT * k + NKT)
                sp.wait_ge(k_fill, PARTS * k + PARTS)
                for part in range(PARTS):
                    sp.dma_start(k_parts[bass.ds(PB * k, PB), part, :, :, :].rearrange("b p c n -> p b (c n)"),
                                 k_blk[:, r, part, :, :, :].rearrange("p b c n -> p b (c n)")).then_inc(k_out[r], 16)

            load_block(0, 0)
            load_block(1, 1)
            with sp.Fori(0, NBLOCK // 2 - 1) as h:
                for r in range(2):
                    store_block(2 * h + r, r)
                    sp.wait_ge(v_proj, SVT + NVT * (2 * h + r) + NVT)
                    load_block(2 * h + r + 2, r)
            for r in range(2):
                store_block(NBLOCK - 2 + r, r)
            for r in range(2):
                sp.wait_ge(k_out[r], 16 * PARTS * NBLOCK // 2)

        @block.tensor
        def _(pe):
            def k_tile(bank, s, src, n, c):
                for k in range(KC):
                    last = nc.tensor.matmul(k_ps[bank][:, 0:n], wk_sb[:, s, k, c * P:(c + 1) * P], src[:, k, :],
                                            start=(k == 0), stop=(k == KC - 1))
                last.then_inc(k_proj, 1)

            def v_tile(bank, s, src, n):
                for k in range(KC):
                    last = nc.tensor.matmul(v_ps[bank][0:n, 0:C], src[:, k, :], wv_sb[:, s, k, :],
                                            start=(k == 0), stop=(k == KC - 1))
                last.then_inc(v_proj, 1)

            pe.wait_ge(small_in, 16)
            t = 0
            for s in (1, 2):
                pe.wait_ge(w_in[s], 32)
                src = small[:, :, (s - 1) * SMALL:s * SMALL]
                for c in range(NC):
                    if t >= KB:
                        pe.wait_ge(k_rest, t - KB + 1)
                    k_tile(t % KB, s, src, SMALL, c)
                    t += 1
                for h in range(2):
                    v_tile(2 * (s - 1) + h, s, src[:, :, h * P:(h + 1) * P], P)
            for s in (0, 3):
                pe.wait_ge(w_in[s], 32)
            with pe.Fori(0, NBLOCK // 2) as h:
                for r in range(2):
                    k = 2 * h + r
                    pe.wait_ge(tok_in[r], 16 * h + 16)
                    for x in range(NKT):
                        c, (b0, nb, col, s) = x // len(KTILES), KTILES[x % len(KTILES)]
                        pe.wait_ge(k_rest, SKT + NKT * k + x - KB + 1)
                        n = nb * SEG[s][1]
                        k_tile(x % KB, s, tok[:, r, :, col:col + n], n, c)
                    for x, (s, col, n, at) in enumerate(VTILES):
                        pe.wait_ge(v_cast, SVT + NVT * k + x - 3)
                        v_tile(x % 4, s, tok[:, r, :, col:col + n], n)

        def small_view(part, s, c):
            return k_small[:, part, c, :, 4 * (s - 1):4 * s]

        def block_view(r, part, c, b0, nb, s):
            return k_blk[:, r, part, b0:b0 + nb, c, SEG[s][0]:SEG[s][0] + SEG[s][1]]

        def keys(ap, s):
            return ap.rearrange("p (b n) -> p b n", n=SEG[s][1])

        @block.scalar
        def _(act):
            def split(t, s, n, bank, hi, mid, rest_at):
                act.wait_ge(k_proj, t + 1)
                nc.scalar.activation(hi, keys(k_ps[bank][:, 0:n], s), ACT.Copy).then_inc(k_hi, 1)
                act.wait_ge(k_rest, t + 1)
                nc.scalar.activation(mid, keys(rest[:, rest_at, 0:n], s), ACT.Copy).then_inc(k_mid, 1)

            for t in range(SKT):
                s, c = 1 + t // NC, t % NC
                split(t, s, SMALL, t % KB, small_view(0, s, c), small_view(1, s, c), t % 2)
            for r in range(2):
                for x in range(NKT):
                    c, (b0, nb, col, s) = x // len(KTILES), KTILES[x % len(KTILES)]
                    split(SKT + NKT * r + x, s, nb * SEG[s][1], x % KB, block_view(r, 0, c, b0, nb, s),
                          block_view(r, 1, c, b0, nb, s), (NKT * r + x) % 2)
            with act.Fori(1, NBLOCK // 2) as h:
                for r in range(2):
                    act.wait_ge(k_out[r], 16 * PARTS * h)
                    for x in range(NKT):
                        c, (b0, nb, col, s) = x // len(KTILES), KTILES[x % len(KTILES)]
                        split(SKT + NKT * (2 * h + r) + x, s, nb * SEG[s][1], x % KB,
                              block_view(r, 0, c, b0, nb, s), block_view(r, 1, c, b0, nb, s), (NKT * r + x) % 2)

        @block.vector
        def _(dve):
            nc.vector.memset(v_pad[:, :, :, :, :], 0.0).then_inc(v_zero, 1)

            def rest_of(t, s, n, bank, hi, rest_at, first=False):
                dve.wait_ge(k_hi, t + 1)
                if not first:
                    dve.wait_ge(k_lo, t - 1)
                nc.vector.tensor_tensor(keys(rest[:, rest_at, 0:n], s), keys(k_ps[bank][:, 0:n], s), hi,
                                        ALU.subtract).then_inc(k_rest, 1)

            def pad(v, bank, buf, n):
                dve.wait_ge(v_proj, v + 1)
                src = v_ps[bank][0:n, 0:C].rearrange("p (g j d) -> p g j d", g=G, j=4)
                nc.vector.tensor_copy(v_pad[0:n, buf, 0:G:2, :, 0:HD], src[:, 0:G:2, :, :])
                nc.vector.tensor_copy(v_pad[0:n, buf, 1:G:2, :, HD:2 * HD], src[:, 1:G:2, :, :]).then_inc(v_cast, 1)

            dve.wait_ge(v_zero, 1)
            for s in (1, 2):
                for c in range(NC):
                    t = NC * (s - 1) + c
                    rest_of(t, s, SMALL, t % KB, small_view(0, s, c), t % 2, t < 2)
                for h in range(2):
                    v = 2 * (s - 1) + h
                    pad(v, v, v, P)
            with dve.Fori(0, NBLOCK // 2) as h:
                for r in range(2):
                    k = 2 * h + r
                    for x in range(NKT):
                        c, (b0, nb, col, s) = x // len(KTILES), KTILES[x % len(KTILES)]
                        rest_of(SKT + NKT * k + x, s, nb * SEG[s][1], x % KB,
                                block_view(r, 0, c, b0, nb, s), (NKT * r + x) % 2)
                    for x, (s, col, n, at) in enumerate(VTILES):
                        dve.wait_ge(v_out[x % NV], 16 * (2 * k + x // NV + 1))
                        pad(SVT + NVT * k + x, x % 4, x % NV, n)

        @block.gpsimd
        def _(pool):
            def low(t, s, n, mid, lo, rest_at):
                pool.wait_ge(k_mid, t + 1)
                nc.gpsimd.tensor_tensor(lo, keys(rest[:, rest_at, 0:n], s), mid, ALU.subtract).then_inc(k_lo, 1)

            def store_v(v, s, buf, row, n):
                pool.wait_ge(v_cast, v + 1)
                pool.dma_start(v_rows[s][bass.ds(row, n), :],
                               v_pad[0:n, buf, :, :, :].rearrange("p g j d -> p (g j d)")).then_inc(v_out[buf], 16)

            for s in (1, 2):
                for c in range(NC):
                    t = NC * (s - 1) + c
                    low(t, s, SMALL, small_view(1, s, c), small_view(2, s, c), t % 2)
                for h in range(2):
                    store_v(2 * (s - 1) + h, s, 2 * (s - 1) + h, h * P, P)
            with pool.Fori(0, NBLOCK // 2) as h:
                for r in range(2):
                    k = 2 * h + r
                    for x in range(NKT):
                        c, (b0, nb, col, s) = x // len(KTILES), KTILES[x % len(KTILES)]
                        low(SKT + NKT * k + x, s, nb * SEG[s][1], block_view(r, 1, c, b0, nb, s),
                            block_view(r, 2, c, b0, nb, s), (NKT * r + x) % 2)
                    for part in range(PARTS):
                        nc.gpsimd.tensor_copy(
                            k_blk[:, r, part, :, :, SEG[1][0]:SEG[1][0] + 8].rearrange("p b c n -> p c b n"),
                            k_small[:, part, :, bass.ds(PB * k, PB), :]).then_inc(k_fill, 1)
                    for x, (s, col, n, at) in enumerate(VTILES):
                        store_v(SVT + NVT * k + x, s, x % NV, (TXT if s == 0 else IPS) * k + at, n)
            for i in range(NV):
                pool.wait_ge(v_out[i], 16 * (1 + NBLOCK * NVT // NV))


def attention_phase(nc, x_t, wq, wo, bias, k_shift, e_den, e_bcast, ident_in, k_parts, v_rows, out_t):
    ctx = ExitStack()
    with ctx:
        def sb(name, shape, dt):
            return ctx.enter_context(nc.sbuf_tensor(name, shape, dt))

        def ps(name, shape, dt):
            return ctx.enter_context(nc.psum_tensor(name, shape, dt))

        def sem(name):
            return ctx.enter_context(nc.semaphore(name))

        def ring(name):
            return [sem(f"{name}{i}") for i in range(R)]

        R = 3
        LAST = B - 1 + 4

        wq_sb = sb("wq_sb", [P, NC, NC, P], F32)
        wo_sb = sb("wo_sb", [P, NC, C], F32)
        bias_sb = sb("bias_sb", [P, NC], F32)
        den_sb = sb("den_sb", [NKEY, G, 32], F32)
        bcast_sb = sb("bcast_sb", [NROW, G, NKEY], BF16)
        ident = sb("ident", [P, P], BF16)
        x_sb = sb("x_sb", [P, R, NC, S], F32)
        xres = sb("xres", [P, R, NC, S], F32)
        q_part = sb("q_part", [P, R, PARTS, NC, S], BF16)
        q_rest = sb("q_rest", [P, NC, S], F32)
        q_stack = sb("q_stack", [NROW + SHIFT, R, SLOTS, S], BF16)
        k_stack = sb("k_stack", [NROW + SHIFT, R, SLOTS, NKEY], BF16)
        v_sb = sb("v_sb", [NKEY, R, HEADS, 32], F32)
        m_sb = sb("m_sb", [P, R, 2, NSEG, SLOTS], F32)
        m_rest = sb("m_rest", [P, 2, NSEG * SLOTS], F32)
        m_part = sb("m_part", [P, PARTS, 2, NSEG * SLOTS], BF16)
        m_t = sb("m_t", [NSEG * SLOTS, PARTS, S], BF16)
        p_sb = sb("p_sb", [NKEY, R, HEADS, S], F32)
        den = sb("den", [P, S], F32)
        inv = sb("inv", [P, S], F32)
        inv_rest = sb("inv_rest", [P, S], F32)
        inv_part = sb("inv_part", [P, PARTS, S], BF16)
        inv_stack = sb("inv_stack", [NROW, R, 4, S], BF16)
        att = sb("att", [P, R, NC, S], F32)
        o_sb = sb("o_sb", [P, R, NC, S], F32)

        a_ps = ps("a_ps", [P, 2, 512], F32)
        b_ps = ps("b_ps", [P, 2, S], F32)
        r_ps = ps("r_ps", [P, 2, S], F32)
        q_ps = ps("q_ps", [P, 512], F32)
        d_ps = ps("d_ps", [P, 512], F32)
        t_ps = ps("t_ps", [P, 512], F32)
        o_ps = ps("o_ps", [P, 512], F32)
        mt_ps = q_ps[0:NSEG * SLOTS, 0:PARTS * S // 2].bitcast(BF16).rearrange("p (a q) -> p a q", a=PARTS)

        consts_in = sem("consts_in")
        zeroed = sem("zeroed")
        x_in, k_in, v_in, xres_in = ring("x_in"), ring("k_in"), ring("v_in"), ring("xres_in")
        q_in, m_in = ring("q_in"), ring("m_in")
        stored = ring("stored")
        q_done = sem("q_done")
        q_hi, q_mid = sem("q_hi"), sem("q_mid")
        q_left = sem("q_left")
        q_lo = sem("q_lo")
        a_done = sem("a_done")
        max_done = sem("max_done")
        m_hi, m_mid = sem("m_hi"), sem("m_mid")
        m_left, m_lo = sem("m_left"), sem("m_lo")
        mt_done = sem("mt_done")
        mt_copied = sem("mt_copied")
        b_done = sem("b_done")
        exp_done = sem("exp_done")
        d_done = sem("d_done")
        d_copied = sem("d_copied")
        recip_done = sem("recip_done")
        i_hi, i_mid = sem("i_hi"), sem("i_mid")
        i_left, i_lo = sem("i_left"), sem("i_lo")
        i_stacked = sem("i_stacked")
        r_done = sem("r_done")
        p_done = sem("p_done")
        v_done = sem("v_done")
        t_copied = sem("t_copied")
        o_done = sem("o_done")
        out_done = sem("out_done")

        block = ctx.enter_context(nc.Block())

        class Step:

            def __init__(self, g, r):
                self.g, self.r, self.known = g, r, isinstance(g, int)

            def live(self, k):
                return not self.known or 0 <= 3 * self.g + self.r - k < B

            def since(self, k, n):
                return not self.known or 3 * self.g + self.r - k >= n

            def batch(self, k):
                return 3 * self.g + (self.r - k)

            def buf(self, k):
                return (self.r - k) % R

            def turn(self, k):
                return self.g + (self.r - k) // R

        FIRST = 2
        LOOPED = B // R

        def run(eng, iteration):
            for g in range(FIRST):
                for r in range(R):
                    iteration(Step(g, r))
            with eng.Fori(FIRST, LOOPED) as g:
                for r in range(R):
                    iteration(Step(g, r))
            for i in range(LOOPED * R, LAST + 1):
                iteration(Step(i // R, i % R))

        Q_AT = {0: (0, 1, 2), 1: (3, 4), 2: (5,), 3: (6, 7, 8)}
        Q_CHUNK = {0: 0, 2: 1, 3: 2}
        O_AT = {5: (0, 1, 2), 6: (3, 4), 7: (5,), 8: (6, 7), 9: (8,)}
        O_CHUNK = {5: 0, 7: 1, 9: 2}
        A_AT = {8: (0, 0), 9: (0, 1), 1: (1, 2), 3: (1, 3), 5: (1, 4)}
        MT_AT = 7
        A_BANKS = [((0, 0), (0, 1)), ((0, 2), (0, 3)), ((1, 0), (1, 1)), ((1, 2), (1, 3)), ((0, 4), (1, 4))]

        def norm_at(w):
            return (3, w - 4) if w >= 4 else (4, w + 6)

        def pv_at(w):
            return (3, w - 5) if w >= 5 else (4, w + 5)

        def rows_of(c):
            return P if c < 2 else C - 2 * P

        @block.sync
        def _(sp):
            def load_x(dst, src, b, buf, done):
                sp.dma_start(dst[:, buf, 0:2, :], src[bass.ds(b, 1), 0:2 * P, :].rearrange("o (c p) q -> p (o c) q", p=P)).then_inc(done, 16)
                sp.dma_start(dst[0:C - 2 * P, buf, 2, :], src[bass.ds(b, 1), 2 * P:C, :].rearrange("o p q -> (o p) q")).then_inc(done, 16)

            load_x(x_sb, x_t, 0, 0, x_in[0])
            sp.dma_start(wq_sb[:, 0:2, :, :].rearrange("p k c m -> p k (c m)"), wq[0:2 * P, :].rearrange("(k p) n -> p k n", p=P)).then_inc(consts_in, 16)
            sp.dma_start(wq_sb[0:C - 2 * P, 2, :, :].rearrange("p c m -> p (c m)"), wq[2 * P:C, :]).then_inc(consts_in, 16)
            sp.dma_start(ident[:, :], ident_in).then_inc(consts_in, 16)
            sp.dma_start(den_sb[:, :, :], e_den).then_inc(consts_in, 16)
            sp.dma_start(bcast_sb[:, :, :], e_bcast).then_inc(consts_in, 16)
            for i in range(R):
                sp.dma_start(k_stack[NROW:, i, :, :], k_shift).then_inc(consts_in, 16)
            sp.dma_start(wo_sb[:, :, :], wo.rearrange("c p n -> p c n")).then_inc(consts_in, 16)
            with nc.allow_non_contiguous_dma(reason="320 biases, once"):
                sp.dma_start(bias_sb[:, 0:2], bias[0:2 * P].rearrange("(c p) -> p c", p=P)).then_inc(consts_in, 16)
                sp.dma_start(bias_sb[0:C - 2 * P, 2:3], bias[2 * P:C].rearrange("(p c) -> p c", c=1)).then_inc(consts_in, 16)

            def iteration(s):
                if s.live(-1):
                    if s.since(-1, R):
                        sp.wait_ge(q_done, 3 * s.batch(-1) - 3 * R + 3)
                    load_x(x_sb, x_t, s.batch(-1), s.buf(-1), x_in[s.buf(-1)])
                if s.live(0):
                    b, i = s.batch(0), s.buf(0)
                    if s.since(0, R):
                        sp.wait_ge(b_done, UNITS * b - UNITS * R + UNITS)
                    row = 0
                    for n in (3, 2, 1):
                        sp.dma_start(k_stack[row:row + n * HD, i, :, :].rearrange("r s n -> r (s n)"),
                                     k_parts[bass.ds(b, 1), 0:n, :, :, :].rearrange("o a (d h) c n -> (o a d) (h c n)", d=HD)).then_inc(k_in[i], 16)
                        row += n * HD
                if s.live(0):
                    b, i = s.batch(0), s.buf(0)
                    sp.wait_ge(q_lo, 3 * b + 3)
                    for row, part in enumerate(QPART):
                        sp.dma_start(q_stack[row * HD:(row + 1) * HD, i, :, :], q_part[:, i, part, :, :]).then_inc(q_in[i], 16)
                if s.live(1):
                    b, i = s.batch(1), s.buf(1)
                    if s.since(1, R):
                        sp.wait_ge(v_done, UNITS * b - UNITS * R + UNITS)
                    for (at, n), rows in zip(SEG, v_rows):
                        sp.dma_start(v_sb[at:at + n, i, :, :].rearrange("p h d -> p (h d)"), rows[bass.ds(n * b, n), :]).then_inc(v_in[i], 16)
                if s.live(3):
                    b, i = s.batch(3), s.buf(3)
                    if s.since(3, R):
                        sp.wait_ge(out_done, 3 * b - 3 * R + 3)
                    load_x(xres, x_t, b, i, xres_in[i])
                if s.live(1):
                    b, i = s.batch(1), s.buf(1)
                    sp.wait_ge(mt_copied, b + 1)
                    for part in range(PARTS):
                        row = NROW + NSEG * part
                        sp.dma_start(q_stack[row:row + NSEG, i, :, :], m_t[:, part, :]).then_inc(m_in[i], 16)
                if s.live(4):
                    b, i = s.batch(4), s.buf(4)
                    sp.wait_ge(out_done, 3 * b + 3)
                    sp.dma_start(out_t[bass.ds(b, 1), 0:2 * P, :].rearrange("o (c p) q -> p (o c) q", p=P), o_sb[:, i, 0:2, :]).then_inc(stored[i], 16)
                    sp.dma_start(out_t[bass.ds(b, 1), 2 * P:C, :].rearrange("o p q -> (o p) q"), o_sb[0:C - 2 * P, i, 2, :]).then_inc(stored[i], 16)

            run(sp, iteration)
            for i in range(R):
                sp.wait_ge(stored[i], 32 * len(range(i, B, R)))

        NCONST = 16 * (5 + R + 3)

        @block.tensor
        def _(pe):
            def project_q(s, x):
                c, k = divmod(x, NC)
                b, i = s.batch(0), s.buf(0)
                if x == 0:
                    pe.wait_ge(x_in[i], 32 * s.turn(0) + 32)
                    if s.since(0, 2):
                        pe.wait_ge(mt_copied, b - 1)
                elif k == 0:
                    pe.wait_ge(q_left, 3 * b + c)
                n = rows_of(k)
                last = nc.tensor.matmul(q_ps[:, 0:S], wq_sb[0:n, k, c, :], x_sb[0:n, i, k, :],
                                        start=(k == 0), stop=(k == NC - 1))
                if k == NC - 1:
                    last.then_inc(q_done, 1)

            def scores_for_max(s, k, a):
                b, i = s.batch(k), s.buf(k)
                if a == 0:
                    pe.wait_ge(q_in[i], 16 * len(QPART) * (s.turn(k) + 1))
                    pe.wait_ge(k_in[i], 48 * (s.turn(k) + 1))
                if a > 0 or s.since(k, 1):
                    pe.wait_ge(max_done, 5 * b + a)
                for bank, (half, g) in enumerate(A_BANKS[a]):
                    for j in range(4):
                        at = slot(4 * g + j)
                        last = nc.tensor.matmul(a_ps[:, bank, j * NKEY:(j + 1) * NKEY],
                                                q_stack[0:NROW, i, at, half * P:(half + 1) * P],
                                                k_stack[0:NROW, i, at, :], start=True, stop=True)
                last.then_inc(a_done, 1)

            def transpose_max(s):
                b = s.batch(1)
                pe.wait_ge(m_lo, b + 1)
                if s.live(0):
                    pe.wait_ge(q_left, 3 * b + 6)
                for part in range(PARTS):
                    for half in range(2):
                        last = nc.tensor.transpose(mt_ps[:, part, half * P:(half + 1) * P], m_part[:, part, half, :], ident[:, :])
                last.then_inc(mt_done, 1)

            def scores(s, u):
                b, i = s.batch(2), s.buf(2)
                if u == 0:
                    pe.wait_ge(m_in[i], 48 * (s.turn(2) + 1))
                if u > 0 or s.since(2, 1):
                    pe.wait_ge(exp_done, UNITS * b + u)
                for h in range(2):
                    at = slot(2 * u + h)
                    last = nc.tensor.matmul(b_ps[0:NKEY, h, :], k_stack[:, i, at, :], q_stack[:, i, at, :], start=True, stop=True)
                last.then_inc(b_done, 1)

            def reciprocals(s, k, u):
                b, i = s.batch(k), s.buf(k)
                if u == 0:
                    pe.wait_ge(i_stacked, b + 1)
                if u > 0 or s.since(k, 1):
                    pe.wait_ge(p_done, UNITS * b + u)
                for h in range(2):
                    g, j = divmod(2 * u + h, 4)
                    last = nc.tensor.matmul(r_ps[0:NKEY, h, :], bcast_sb[:, g, :], inv_stack[:, i, j, :], start=True, stop=True)
                last.then_inc(r_done, 1)

            def denominators(s, u):
                b, i = s.batch(2), s.buf(2)
                pe.wait_ge(exp_done, UNITS * b + u + 1)
                if u == 0 and s.since(2, 1):
                    pe.wait_ge(d_copied, b)
                for h in range(2):
                    g, j = divmod(2 * u + h, 4)
                    last = nc.tensor.matmul(d_ps[32 * j:32 * j + 32, 0:S], den_sb[:, g, :], p_sb[:, i, 2 * u + h, :],
                                            start=(g == 0), stop=(g == G - 1), tile_position=(0, 32 * j), skip_group_check=True)
                if u == UNITS - 1:
                    last.then_inc(d_done, 1)

            def attend(s, k, u):
                b, i = s.batch(k), s.buf(k)
                pe.wait_ge(p_done, UNITS * b + u + 1)
                if u == 0:
                    pe.wait_ge(v_in[i], 64 * (s.turn(k) + 1))
                if u in (0, 4, 8) and (u > 0 or s.since(k, 1)):
                    pe.wait_ge(t_copied, 3 * b + u // 4)
                for h in range(2):
                    g, j = divmod(2 * u + h, 4)
                    last = nc.tensor.matmul(t_ps[32 * j:32 * j + 32, 0:S], v_sb[:, i, 2 * u + h, :], p_sb[:, i, 2 * u + h, :],
                                            start=(g % 2 == 0), stop=(g % 2 == 1 or g == G - 1), tile_position=(0, 32 * j), skip_group_check=True)
                last.then_inc(v_done, 1)

            def project_out(s, x):
                c, k = divmod(x, NC)
                b, i = s.batch(4), s.buf(4)
                if x == 0:
                    pe.wait_ge(t_copied, 3 * b + 3)
                if k == 0 and (c > 0 or s.since(4, 1)):
                    pe.wait_ge(out_done, 3 * b + c)
                m = rows_of(c)
                last = nc.tensor.matmul(o_ps[0:m, 0:S], wo_sb[:, k, c * P:c * P + m], att[:, i, k, :],
                                        start=(k == 0), stop=(k == NC - 1))
                if k == NC - 1:
                    last.then_inc(o_done, 1)

            def iteration(s):
                for w in range(UNITS):
                    if s.live(2):
                        scores(s, w)
                    k, u = norm_at(w)
                    if s.live(k):
                        reciprocals(s, k, u)
                    if s.live(0):
                        for x in Q_AT.get(w, ()):
                            project_q(s, x)
                    if w in A_AT and s.live(A_AT[w][0]):
                        scores_for_max(s, *A_AT[w])
                    if s.live(4):
                        for x in O_AT.get(w, ()):
                            project_out(s, x)
                    if w == MT_AT and s.live(1):
                        transpose_max(s)
                    if s.live(2):
                        denominators(s, w)
                    k, u = pv_at(w)
                    if s.live(k):
                        attend(s, k, u)

            pe.wait_ge(consts_in, NCONST)
            run(pe, iteration)

        @block.scalar
        def _(act):
            def high_q(s, c):
                b, i = s.batch(0), s.buf(0)
                act.wait_ge(q_done, 3 * b + c + 1)
                if c == 0 and s.since(0, R):
                    act.wait_ge(q_in[i], 16 * len(QPART) * s.turn(0))
                nc.scalar.activation(q_part[:, i, 0, c, :], q_ps[:, 0:S], ACT.Copy).then_inc(q_hi, 1)

            def mid_q(s, c):
                b, i = s.batch(0), s.buf(0)
                act.wait_ge(q_left, 3 * b + c + 1)
                nc.scalar.activation(q_part[:, i, 1, c, :], q_rest[:, c, :], ACT.Copy).then_inc(q_mid, 1)

            def exponentials(s, u):
                b, i = s.batch(2), s.buf(2)
                act.wait_ge(b_done, UNITS * b + u + 1)
                if u == 0 and s.since(2, R):
                    act.wait_ge(v_done, UNITS * b - UNITS * R + UNITS)
                nc.scalar.activation(p_sb[:, i, 2 * u:2 * u + 2, :], b_ps[0:NKEY, :, :], ACT.Exp, scale=SCALE).then_inc(exp_done, 1)

            def split_max(s):
                b, i = s.batch(1), s.buf(1)
                act.wait_ge(max_done, 5 * b + 5)
                if s.since(1, 1):
                    act.wait_ge(mt_done, b)
                nc.scalar.activation(m_part[:, 0, :, :], m_sb[:, i, :, :, :].rearrange("p a s h -> p a (s h)"), ACT.Copy).then_inc(m_hi, 1)
                act.wait_ge(m_left, b + 1)
                nc.scalar.activation(m_part[:, 1, :, :], m_rest[:, :, :], ACT.Copy).then_inc(m_mid, 1)

            def copy_max(s):
                b = s.batch(1)
                act.wait_ge(mt_done, b + 1)
                if s.since(1, 1):
                    act.wait_ge(m_in[s.buf(2)], 48 * (s.turn(2) + 1))
                nc.scalar.activation(m_t[:, :, :], mt_ps, ACT.Copy).then_inc(mt_copied, 1)

            def copy_den(s):
                b = s.batch(3)
                act.wait_ge(d_done, b + 1)
                if s.since(3, 1):
                    act.wait_ge(recip_done, b)
                nc.scalar.activation(den[:, :], d_ps[:, 0:S], ACT.Copy).then_inc(d_copied, 1)

            def high_inv(s):
                b = s.batch(3)
                act.wait_ge(recip_done, b + 1)
                if s.since(3, 1):
                    act.wait_ge(i_stacked, b)
                nc.scalar.activation(inv_part[:, 0, :], inv[:, :], ACT.Copy).then_inc(i_hi, 1)

            def mid_inv(s):
                b = s.batch(3)
                act.wait_ge(i_left, b + 1)
                nc.scalar.activation(inv_part[:, 1, :], inv_rest[:, :], ACT.Copy).then_inc(i_mid, 1)

            def copy_attention(s, k, c):
                b, i = s.batch(k), s.buf(k)
                act.wait_ge(v_done, UNITS * b + (4, 8, 10)[c])
                if c == 0 and s.since(k, R):
                    act.wait_ge(o_done, 3 * b - 3 * R + 3)
                nc.scalar.activation(att[:, i, c, :], t_ps[:, 0:S], ACT.Copy).then_inc(t_copied, 1)

            def iteration(s):
                for w in range(UNITS):
                    if w == 0 and s.live(3):
                        copy_den(s)
                    if s.live(2):
                        exponentials(s, w)
                    if w == 1 and s.live(3):
                        high_inv(s)
                    if w in Q_CHUNK and s.live(0):
                        high_q(s, Q_CHUNK[w])
                    if w == 1 and s.live(3):
                        mid_inv(s)
                    if w in Q_CHUNK and s.live(0):
                        mid_q(s, Q_CHUNK[w])
                    if w == MT_AT - 1 and s.live(1):
                        split_max(s)
                    if w == MT_AT and s.live(1):
                        copy_max(s)
                    for at, k, c in ((8, 3, 0), (2, 4, 1), (4, 4, 2)):
                        if w == at and s.live(k):
                            copy_attention(s, k, c)

            run(act, iteration)

        @block.vector
        def _(dve):
            for i in range(R):
                nc.vector.memset(m_sb[:, i, :, :, :], 0.0).then_inc(zeroed, 1)

            def left_q(s, c):
                b, i = s.batch(0), s.buf(0)
                dve.wait_ge(q_hi, 3 * b + c + 1)
                if s.since(0, 1):
                    dve.wait_ge(q_lo, 3 * b - 3 + c + 1)
                nc.vector.tensor_tensor(q_rest[:, c, :], q_ps[:, 0:S], q_part[:, i, 0, c, :], ALU.subtract).then_inc(q_left, 1)

            def maxima(s, k, a):
                b, i = s.batch(k), s.buf(k)
                dve.wait_ge(a_done, 5 * b + a + 1)
                if a == 0 and s.since(k, R):
                    dve.wait_ge(m_left, b - R + 1)
                src = a_ps[:, :, 0:4 * NKEY].rearrange("p a (j n) -> p a j n", j=4)
                (h0, g0), (h1, g1) = A_BANKS[a]

                def dst(s0, s1):
                    m = m_sb[:, i, :, s0:s1, :].rearrange("p q s (e j c) -> p q e j c s", e=2, j=4)
                    if h0 == h1:
                        return m[:, h0, :, :, g0 // 2, :]
                    return m[:, :, 0, :, g0 // 2, :]

                for first, count in ((0, 1), (3, 1)):
                    at, n = SEG[first]
                    nc.vector.tensor_reduce(dst(first, first + 1), src[:, :, :, at:at + n], AX.X, ALU.max)
                at, n = SEG[1]
                small = src[:, :, :, at:at + 2 * n].rearrange("p a j (s n) -> p a j s n", s=2)
                nc.vector.tensor_reduce(dst(1, 3), small, AX.X, ALU.max).then_inc(max_done, 1)

            def invert(s):
                b = s.batch(3)
                dve.wait_ge(d_copied, b + 1)
                if s.since(3, 1):
                    dve.wait_ge(i_left, b)
                nc.vector.reciprocal(inv[:, :], den[:, :]).then_inc(recip_done, 1)

            def left_inv(s):
                b = s.batch(3)
                dve.wait_ge(i_hi, b + 1)
                if s.since(3, 1):
                    dve.wait_ge(i_lo, b)
                nc.vector.tensor_tensor(inv_rest[:, :], inv[:, :], inv_part[:, 0, :], ALU.subtract).then_inc(i_left, 1)

            def low_inv(s):
                b = s.batch(3)
                dve.wait_ge(i_mid, b + 1)
                nc.vector.tensor_tensor(inv_part[:, 2, :], inv_rest[:, :], inv_part[:, 1, :], ALU.subtract).then_inc(i_lo, 1)

            def stack_inv(s):
                b, i = s.batch(3), s.buf(3)
                dve.wait_ge(i_lo, b + 1)
                if s.since(3, R):
                    dve.wait_ge(r_done, UNITS * b - UNITS * R + UNITS)
                for part in range(PARTS):
                    for j in range(4):
                        last = nc.vector.tensor_copy(inv_stack[32 * part:32 * part + 32, i, j, :], inv_part[32 * j:32 * j + 32, part, :])
                last.then_inc(i_stacked, 1)

            def normalise(s, k, u):
                b, i = s.batch(k), s.buf(k)
                dve.wait_ge(r_done, UNITS * b + u + 1)
                both = p_sb[:, i, 2 * u:2 * u + 2, :]
                nc.vector.tensor_tensor(both, r_ps[0:NKEY, :, :], both, ALU.mult).then_inc(p_done, 1)

            def finish(s, c):
                b, i = s.batch(4), s.buf(4)
                dve.wait_ge(o_done, 3 * b + c + 1)
                if c == 0:
                    dve.wait_ge(xres_in[i], 32 * (s.turn(4) + 1))
                    if s.since(4, R):
                        dve.wait_ge(stored[i], 32 * s.turn(4))
                m = rows_of(c)
                nc.vector.scalar_tensor_tensor(out=o_sb[0:m, i, c, :], in0=o_ps[0:m, 0:S], scalar=bias_sb[0:m, c:c + 1],
                                               in1=xres[0:m, i, c, :], op0=ALU.add, op1=ALU.add).then_inc(out_done, 1)

            def iteration(s):
                for w in range(UNITS):
                    k, u = norm_at(w)
                    if s.live(k):
                        normalise(s, k, u)
                    if w in Q_CHUNK and s.live(0):
                        left_q(s, Q_CHUNK[w])
                    if w == 0 and s.live(3):
                        invert(s)
                    if w == 1 and s.live(3):
                        left_inv(s)
                    if w == 2 and s.live(3):
                        low_inv(s)
                        stack_inv(s)
                    if w in A_AT and s.live(A_AT[w][0]):
                        maxima(s, *A_AT[w])
                    if w in O_CHUNK and s.live(4):
                        finish(s, O_CHUNK[w])

            dve.wait_ge(consts_in, NCONST)
            dve.wait_ge(zeroed, R)
            run(dve, iteration)

        @block.gpsimd
        def _(pool):
            def low_q(s, c):
                b, i = s.batch(0), s.buf(0)
                pool.wait_ge(q_mid, 3 * b + c + 1)
                nc.gpsimd.tensor_tensor(q_part[:, i, 2, c, :], q_rest[:, c, :], q_part[:, i, 1, c, :], ALU.subtract).then_inc(q_lo, 1)

            def low_max(s):
                b, i = s.batch(1), s.buf(1)
                pool.wait_ge(m_hi, b + 1)
                if s.since(1, 1):
                    pool.wait_ge(m_lo, b)
                nc.gpsimd.tensor_tensor(m_rest[:, :, :], m_sb[:, i, :, :, :].rearrange("p a s h -> p a (s h)"),
                                        m_part[:, 0, :, :], ALU.subtract).then_inc(m_left, 1)
                pool.wait_ge(m_mid, b + 1)
                nc.gpsimd.tensor_tensor(m_part[:, 2, :, :], m_rest[:, :, :], m_part[:, 1, :, :], ALU.subtract).then_inc(m_lo, 1)

            def iteration(s):
                for w in range(UNITS):
                    if w in Q_CHUNK and s.live(0):
                        low_q(s, Q_CHUNK[w])
                    if w == MT_AT - 1 and s.live(1):
                        low_max(s)

            run(pool, iteration)


def cross_attention(nc, a, out_t):
    k_parts = nc.dram_tensor("k_parts", [B, PARTS, P, NC, NKEY], BF16, kind="Internal").ap()
    v_rows = [nc.dram_tensor(f"v_rows{s}", [B * n, HEADS * 32], F32, kind="Internal").ap() for s, (_, n) in enumerate(SEG)]
    context_phase(nc, a["ctx_main"], a["ctx_small"], [a[f"wk{s}"] for s in range(NSEG)], [a[f"wv{s}"] for s in range(NSEG)],
                  k_parts, v_rows)
    attention_phase(nc, a["x_t"], a["wq"], a["wo"], a["bias"], a["k_shift"], a["e_den"], a["e_bcast"], a["ident"],
                    k_parts, v_rows, out_t)


def constants():
    import numpy as np
    bf = np.dtype("bfloat16")
    k_shift = np.zeros((PARTS, NSEG, SLOTS, NKEY), bf)
    e_den = np.zeros((NKEY, G, 32), np.float32)
    e_den[:, 0, 4 * G:] = 1.0
    e_bcast = np.zeros((PARTS, 32, G, NKEY), bf)
    for s, (at, n) in enumerate(SEG):
        k_shift[:, s, :, at:at + n] = -1.0
        for g in range(G):
            e_den[at:at + n, g, 4 * g + s] = 1.0
            e_bcast[:, 4 * g + s, g, at:at + n] = 1.0
    return {
        "k_shift": k_shift.reshape(SHIFT, SLOTS, NKEY), "e_den": e_den,
        "e_bcast": e_bcast.reshape(NROW, G, NKEY), "ident": np.eye(P, dtype=bf),
    }


def kernel(**inputs):
    import numpy as np
    import concourse.bacc as bacc
    from concourse.bass_utils import run_bass_kernel_spmd

    w = {n[len("L0_xattn_to_"):]: np.asarray(v) for n, v in inputs.items() if n.startswith("L0_")}
    x, context = np.asarray(inputs["x"]), np.asarray(inputs["ctx_2048"])

    def head_columns(m):
        full = np.zeros((m.shape[0], NC * 8, HD), m.dtype)
        full[:, :HEADS] = m.reshape(-1, HEADS, HD)
        return np.ascontiguousarray(full.reshape(-1, NC, 8, HD).transpose(0, 1, 3, 2)).reshape(-1, NC * P)

    def tokens(first, n, batches):
        part = context[:, first:first + n].reshape(B // batches, batches * n, CTX)
        return part.transpose(0, 2, 1)

    wo = np.zeros((2 * NC, 4, HD, C), w["out_w"].dtype)
    wo[:G] = w["out_w"].reshape(G, 4, HD, C)
    wo = wo.reshape(NC, 2, 4, HD, C).transpose(0, 2, 1, 3, 4)
    arrays = {
        "x_t": x.transpose(0, 2, 1),
        "ctx_main": np.concatenate([tokens(*SEG[0], PB), tokens(*SEG[3], PB)], axis=2),
        "ctx_small": np.concatenate([tokens(*SEG[1], B)[0], tokens(*SEG[2], B)[0]], axis=1),
        "wq": head_columns(w["q_w"]), "wo": wo.reshape(NC, P, C), "bias": w["out_b"],
    }
    for s, name in enumerate(("", "_object", "_others", "_ip")):
        arrays[f"wk{s}"] = head_columns(w[f"k{name}_w"])
        arrays[f"wv{s}"] = w[f"v{name}_w"]
    arrays.update(constants())
    arrays = {n: np.ascontiguousarray(v) for n, v in arrays.items()}

    nc = bacc.Bacc("TRN2", target_bir_lowering=False, num_devices=1)
    aps = {n: nc.dram_tensor(f"in_{n}", v.shape, mybir.dt.from_np(v.dtype), kind="ExternalInput").ap() for n, v in arrays.items()}
    out = nc.dram_tensor("out_t", (B, C, S), F32, kind="ExternalOutput").ap()
    cross_attention(nc, aps, out)
    r = run_bass_kernel_spmd(nc, [{f"in_{n}": v for n, v in arrays.items()}], core_ids=[0])
    return r.results[0]["out_t"].transpose(0, 2, 1)
```

```python
import concourse.bass as bass
from concourse import mybir
from contextlib import ExitStack

F32 = mybir.dt.float32
F32R = mybir.dt.float32r
BF16 = mybir.dt.bfloat16
ALU = mybir.AluOpType
ACT = mybir.ActivationFunctionType
AX = mybir.AxisListType

B, S, C = 64, 256, 320
CTX, NKEY = 512, 120
HEADS, HD = 20, 16
SEG = [(0, 77), (77, 4), (81, 4), (85, 35)]
NSEG = len(SEG)
SCALE = HD ** -0.5

P = 128
G = 5
NC = 3
SLOTS = 8 * NC
PARTS = 3
QPART = [0, 0, 0, 1, 1, 2]
NROW = HD * len(QPART)
SHIFT = PARTS * NSEG
UNITS = 10

KC = CTX // P
PB = 8
NBLOCK = B // PB
TXT, IPS = PB * SEG[0][1], PB * SEG[3][1]
TOK = TXT + IPS
SMALL = B * SEG[1][1]
KTILES = [(c, 0, PB, 3) for c in range(NC)] + [(c, b0, PB // 2, 0) for c in range(NC) for b0 in (0, PB // 2)]


def tiles_of(first, count):
    return [(at, min(first + count - at, P)) for at in range(first, first + count, P)]


VTILES = [(3, *t) for t in tiles_of(0, IPS)] + [(0, *t) for t in tiles_of(0, TXT)]
NV = 4
KB = 3


SCORES = 21
DENS = 21
NORMS = 35
ATTENDS = 36
X_AT = -6
Q_AT = (0, 0, 0, 1, 1, 1, 2, 2, 3)
MAX_AT = (9, 10, 11, 13, 14)
MT_AT = 17
T_COPY = (39, 43, 45)
O_AT = (46, 47, 48, 49, 51, 52, 54, 55, 55)
Q_HIGH, Q_LEFT, Q_MID = (0, 1, 3), (1, 1, 3), (1, 1, 4)
MAX_HIGH, MAX_MID = 15, 16
DEN_COPY, INVERT, INV_HIGH, INV_MID, INV_LOW, INV_STACK = 31, 31, 32, 32, 32, 33
LATEST = 5


def due(times, w):
    return [(t // UNITS, x) for x, t in enumerate(times) if t % UNITS == w]


def pairs(first):
    return tuple(range(first, first + UNITS))


def slot(n):
    g, j = divmod(n, 4)
    return 3 * (4 * (g % 2) + j) + g // 2


def constant_tensors(nc, ctx):
    def sb(name, shape, dt):
        return ctx.enter_context(nc.sbuf_tensor(name, shape, dt))

    return {
        "wq_hi": sb("wq_hi", [P, NC, NC * P], F32R),
        "wq_lo": sb("wq_lo", [P, NC, NC * P], F32R),
        "wo_hi": sb("wo_hi", [P, NC, C], F32R),
        "wo_lo": sb("wo_lo", [P, NC, C], F32R),
        "bias": sb("bias_sb", [P, NC], F32),
        "e_den": sb("den_sb", [NKEY, G, 32], F32),
        "e_bcast": sb("bcast_sb", [NROW, G, NKEY], BF16),
        "ident": sb("ident_sb", [P, P], BF16),
    }


def context_phase(nc, ctx_txt, ctx_ip, ctx_small, wk, wv, source, const, k_parts, v_rows):
    ctx = ExitStack()
    with ctx:
        def sb(name, shape, dt):
            return ctx.enter_context(nc.sbuf_tensor(name, shape, dt))

        def sem(name):
            return ctx.enter_context(nc.semaphore(name))

        wk_hi = sb("wk_hi", [P, NSEG, KC, NC * P], F32R)
        wk_lo = sb("wk_lo", [P, NSEG, KC, NC * P], F32R)
        wv_hi = sb("wv_hi", [P, NSEG, KC, C], F32R)
        wv_lo = sb("wv_lo", [P, NSEG, KC, C], F32R)
        staged = sb("staged", [P, KC * TOK], F32)
        txt_hi = sb("txt_hi", [P, KC * TXT], F32R)
        txt_lo = sb("txt_lo", [P, KC * TXT], F32R)
        ip_hi = sb("ip_hi", [P, KC, IPS], F32R)
        ip_lo = sb("ip_lo", [P, KC, IPS], F32R)
        halves = sb("halves", [P, 2], F32)
        k_small = sb("k_small", [P, PARTS, NC, B, 8], BF16)
        k_blk = sb("k_blk", [P, 2, PARTS, PB, NC, NKEY], BF16)
        rest = sb("rest", [P, 2, 512], F32)
        v_pad = sb("v_pad", [P, NV, G, 4, 32], F32)
        k_ps = [ctx.enter_context(nc.psum_tensor(f"k_ps{i}", [P, 512], F32)) for i in range(KB)]
        v_ps = [ctx.enter_context(nc.psum_tensor(f"v_ps{i}", [P, 512], F32)) for i in range(4)]

        def chunks(ap):
            return ap.rearrange("p (k n) -> p k n", k=KC)

        ip_staged, txt_staged = chunks(staged[:, 0:KC * IPS]), chunks(staged[:, KC * IPS:])
        small_staged = chunks(staged[:, 0:2 * KC * SMALL])
        small_hi, small_lo = chunks(txt_hi[:, 0:2 * KC * SMALL]), chunks(txt_lo[:, 0:2 * KC * SMALL])
        w_staged = [k_blk[:, r, :, :, :, :].rearrange("p a b c n -> p (a b c n)").bitcast(F32) for r in range(2)]
        SPLIT = KC * NC * P
        wk_staged = [chunks(w[:, 0:SPLIT]) for w in w_staged]
        wv_staged = [chunks(w[:, SPLIT:SPLIT + KC * C]) for w in w_staged]

        wq_staged = staged[:, 0:NC * NC * P].rearrange("p (k m) -> p k m", k=NC)
        wo_staged = staged[:, NC * NC * P:NC * NC * P + NC * C].rearrange("p (k n) -> p k n", k=NC)

        consts_in = sem("consts_in")
        proj_high = sem("proj_high")
        proj_low = sem("proj_low")
        w_in = [sem(f"w_in{s}") for s in range(NSEG)]
        w_high = sem("w_high")
        w_low = sem("w_low")
        small_in, small_high, small_low = sem("small_in"), sem("small_high"), sem("small_low")
        ip_in, ip_high, ip_low = sem("ip_in"), sem("ip_high"), sem("ip_low")
        txt_in, txt_high, txt_low = sem("txt_in"), sem("txt_high"), sem("txt_low")
        k_out = [sem("k_out0"), sem("k_out1")]
        v_out = [sem(f"v_out{i}") for i in range(NV)]
        k_proj = sem("k_proj")
        k_hi = sem("k_hi")
        k_rest = sem("k_rest")
        k_mid = sem("k_mid")
        k_lo = sem("k_lo")
        k_fill = sem("k_fill")
        v_proj = sem("v_proj")
        v_cast = sem("v_cast")
        v_zero = sem("v_zero")

        GROUPS = (1, 2, 3, 0)
        NKT, NVT = len(KTILES), len(VTILES)
        IKT, IVT = NC, len(tiles_of(0, IPS))
        SKT, SVT = 2 * NC, 4

        def run_blocks(eng, body):
            with eng.Fori(0, NBLOCK // 2 - 1) as h:
                for r in range(2):
                    body(2 * h + r, r, False)
            for k in (NBLOCK - 2, NBLOCK - 1):
                body(k, k % 2, k == NBLOCK - 1)

        block = ctx.enter_context(nc.Block())

        @block.sync
        def _(sp):
            def load_weights(i):
                s = GROUPS[i]
                if i >= 2:
                    sp.wait_ge(w_low, i - 1)
                sp.dma_start(wk_staged[i % 2], wk[s].rearrange("(k p) n -> p k n", p=P)).then_inc(w_in[s], 16)
                sp.dma_start(wv_staged[i % 2], wv[s].rearrange("(k p) n -> p k n", p=P)).then_inc(w_in[s], 16)

            def load_tokens(k):
                sp.wait_ge(ip_low, k)
                sp.dma_start(ip_staged, ctx_ip[bass.ds(k, 1), :, :].rearrange("o (k p) n -> p (o k) n", p=P)).then_inc(ip_in, 16)
                sp.wait_ge(txt_low, k)
                sp.dma_start(txt_staged, ctx_txt[bass.ds(k, 1), :, :].rearrange("o (k p) n -> p (o k) n", p=P)).then_inc(txt_in, 16)

            def store_v(v, s, buf, row, n):
                sp.wait_ge(v_cast, v + 1)
                sp.dma_start(v_rows[s][bass.ds(row, n), :],
                             v_pad[0:n, buf, :, :, :].rearrange("p g j d -> p (g j d)")).then_inc(v_out[buf], 16)

            def store_block_v(k, x):
                s, at, n = VTILES[x]
                store_v(SVT + NVT * k + x, s, x % NV, (TXT if s == 0 else IPS) * k + at, n)

            def load_constants():
                sp.wait_ge(txt_low, NBLOCK)
                sp.wait_ge(ip_low, NBLOCK)
                wq, wo, bias = source["wq"], source["wo"], source["bias"]
                sp.dma_start(wq_staged[:, 0:2, :], wq[0:2 * P, :].rearrange("(k p) n -> p k n", p=P)).then_inc(consts_in, 16)
                for row in (0, P // 2):
                    sp.dma_start(wq_staged[row:row + P // 2, 2, :], wq[2 * P:C, :]).then_inc(consts_in, 16)
                sp.dma_start(wo_staged, wo.rearrange("c p n -> p c n")).then_inc(consts_in, 16)
                sp.dma_start(halves[:, :], source["wo_rows"]).then_inc(consts_in, 16)
                for name in ("ident", "e_den", "e_bcast"):
                    sp.dma_start(const[name][:], source[name]).then_inc(consts_in, 16)
                with nc.allow_non_contiguous_dma(reason="320 biases, once"):
                    sp.dma_start(const["bias"][:, 0:2], bias[0:2 * P].rearrange("(c p) -> p c", p=P)).then_inc(consts_in, 16)
                    sp.dma_start(const["bias"][0:C - 2 * P, 2:3], bias[2 * P:C].rearrange("(p c) -> p c", c=1)).then_inc(consts_in, 16)

            def step(k, r, last):
                if last:
                    load_constants()
                else:
                    load_tokens(k + 1)
                for x in range(IVT):
                    store_block_v(k, x)
                sp.wait_ge(k_lo, SKT + NKT * k + NKT)
                sp.wait_ge(k_fill, PARTS * k + PARTS)
                for part in range(PARTS):
                    sp.dma_start(k_parts[bass.ds(PB * k, PB), part, :, :, :].rearrange("b p c n -> p b (c n)"),
                                 k_blk[:, r, part, :, :, :].rearrange("p b c n -> p b (c n)")).then_inc(k_out[r], 16)
                for x in range(IVT, NVT):
                    store_block_v(k, x)

            sp.dma_start(small_staged, ctx_small.rearrange("(k p) n -> p k n", p=P)).then_inc(small_in, 16)
            load_weights(0)
            load_weights(1)
            load_weights(2)
            sp.wait_ge(small_low, 1)
            sp.dma_start(ip_staged, ctx_ip[0, :, :].rearrange("(k p) n -> p k n", p=P)).then_inc(ip_in, 16)
            load_weights(3)
            sp.dma_start(txt_staged, ctx_txt[0, :, :].rearrange("(k p) n -> p k n", p=P)).then_inc(txt_in, 16)
            for i, s in enumerate(GROUPS[:2]):
                for h in range(2):
                    store_v(2 * i + h, s, 2 * i + h, h * P, P)
            run_blocks(sp, step)
            for r in range(2):
                sp.wait_ge(k_out[r], 16 * PARTS * NBLOCK // 2)
            for i in range(NV):
                sp.wait_ge(v_out[i], 16 * (1 + NBLOCK * NVT // NV))

        NCONST = 16 * (8 + 2)

        @block.tensor
        def _(pe):
            def product(out, left, right, done):
                for k in range(KC):
                    for at, (x, y) in enumerate(((0, 0), (0, 1), (1, 0))):
                        last = nc.tensor.matmul(out, left[x](k), right[y](k),
                                                start=(k == 0 and at == 0), stop=(k == KC - 1 and at == 2))
                last.then_inc(done, 1)

            def k_tile(bank, s, src, first, n, c):
                product(k_ps[bank][:, 0:n], [lambda k, w=w: w[:, s, k, c * P:(c + 1) * P] for w in (wk_hi, wk_lo)],
                        [lambda k, x=x: x[:, k, first:first + n] for x in src], k_proj)

            def v_tile(bank, s, src, first, n):
                product(v_ps[bank][0:n, 0:C], [lambda k, x=x: x[:, k, first:first + n] for x in src],
                        [lambda k, w=w: w[:, s, k, :] for w in (wv_hi, wv_lo)], v_proj)

            pe.wait_ge(small_low, 1)
            t = 0
            for i, s in enumerate(GROUPS[:2]):
                pe.wait_ge(w_low, i + 1)
                for c in range(NC):
                    if t >= KB:
                        pe.wait_ge(k_rest, t - KB + 1)
                    k_tile(t % KB, s, (small_hi, small_lo), i * SMALL, SMALL, c)
                    t += 1
                for h in range(2):
                    v_tile(2 * i + h, s, (small_hi, small_lo), i * SMALL + h * P, P)
            pe.wait_ge(w_low, 3)

            def step(k, r, last):
                def half(k_tiles, v_tiles, src):
                    for x in k_tiles:
                        c, b0, nb, s = KTILES[x]
                        pe.wait_ge(k_rest, SKT + NKT * k + x - KB + 1)
                        n = SEG[s][1]
                        k_tile(x % KB, s, src, b0 * n, nb * n, c)
                    for x in v_tiles:
                        s, at, n = VTILES[x]
                        pe.wait_ge(v_cast, SVT + NVT * k + x - 3)
                        v_tile(x % 4, s, src, at, n)

                pe.wait_ge(ip_low, k + 1)
                half(range(IKT), range(IVT), (ip_hi, ip_lo))
                pe.wait_ge(txt_low, k + 1)
                pe.wait_ge(w_low, NSEG)
                half(range(IKT, NKT), range(IVT, NVT), (chunks(txt_hi[:, :]), chunks(txt_lo[:, :])))

            run_blocks(pe, step)

        def small_view(part, s, c):
            return k_small[:, part, c, :, 4 * (s - 1):4 * s]

        def block_view(r, part, c, b0, nb, s):
            return k_blk[:, r, part, b0:b0 + nb, c, SEG[s][0]:SEG[s][0] + SEG[s][1]]

        def keys(ap, s):
            return ap.rearrange("p (b n) -> p b n", n=SEG[s][1])

        @block.scalar
        def _(act):
            def split(t, s, n, bank, hi, mid, rest_at):
                act.wait_ge(k_proj, t + 1)
                nc.scalar.activation(hi, keys(k_ps[bank][:, 0:n], s), ACT.Copy).then_inc(k_hi, 1)
                act.wait_ge(k_rest, t + 1)
                nc.scalar.activation(mid, keys(rest[:, rest_at, 0:n], s), ACT.Copy).then_inc(k_mid, 1)

            def high_weights(i):
                s = GROUPS[i]
                act.wait_ge(w_in[s], 32)
                nc.scalar.activation(wk_hi[:, s, :, :], wk_staged[i % 2], ACT.Copy)
                nc.scalar.activation(wv_hi[:, s, :, :], wv_staged[i % 2], ACT.Copy).then_inc(w_high, 1)

            def high_ip(k):
                act.wait_ge(ip_in, 16 * k + 16)
                nc.scalar.activation(ip_hi[:, :, :], ip_staged, ACT.Copy).then_inc(ip_high, 1)

            def small(i):
                s = GROUPS[i]
                for c in range(NC):
                    t = NC * i + c
                    split(t, s, SMALL, t % KB, small_view(0, s, c), small_view(1, s, c), t % 2)

            act.wait_ge(small_in, 16)
            nc.scalar.activation(small_hi, small_staged, ACT.Copy).then_inc(small_high, 1)
            high_weights(0)
            high_weights(1)
            small(0)
            high_weights(2)
            small(1)
            high_ip(0)
            high_weights(3)

            def step(k, r, last, first=False):
                act.wait_ge(k_proj, SKT + NKT * k)
                act.wait_ge(v_proj, SVT + NVT * k)
                act.wait_ge(txt_in, 16 * k + 16)
                nc.scalar.activation(chunks(txt_hi[:, :]), txt_staged, ACT.Copy).then_inc(txt_high, 1)
                if first:
                    act.wait_ge(w_low, 3 + k)
                else:
                    act.wait_ge(k_out[r], 8 * PARTS * (k - r))
                for x, (c, b0, nb, s) in enumerate(KTILES):
                    split(SKT + NKT * k + x, s, nb * SEG[s][1], x % KB, block_view(r, 0, c, b0, nb, s),
                          block_view(r, 1, c, b0, nb, s), (NKT * r + x) % 2)
                    if x == IKT:
                        act.wait_ge(k_lo, SKT)
                        for part in range(PARTS):
                            nc.scalar.activation(
                                k_blk[:, r, part, :, :, SEG[1][0]:SEG[1][0] + 8].rearrange("p b c n -> p c b n"),
                                k_small[:, part, :, bass.ds(PB * k, PB), :], ACT.Copy).then_inc(k_fill, 1)
                if last:
                    act.wait_ge(consts_in, NCONST)
                    nc.scalar.activation(const["wq_hi"][:, :, :], wq_staged, ACT.Copy)
                    nc.scalar.activation(const["wo_hi"][:, :, :], wo_staged, ACT.Copy).then_inc(proj_high, 1)
                else:
                    act.wait_ge(v_proj, SVT + NVT * k + IVT)
                    high_ip(k + 1)

            for k in range(2):
                step(k, k, False, first=True)
            with act.Fori(1, NBLOCK // 2 - 1) as h:
                for r in range(2):
                    step(2 * h + r, r, False)
            for k in (NBLOCK - 2, NBLOCK - 1):
                step(k, k % 2, k == NBLOCK - 1)

        @block.vector
        def _(dve):
            nc.vector.memset(v_pad[:, :, :, :, :], 0.0).then_inc(v_zero, 1)

            def low(out, value, hi, done):
                nc.vector.tensor_tensor(out, value, hi, ALU.subtract).then_inc(done, 1)

            def low_weights(i):
                s = GROUPS[i]
                dve.wait_ge(w_high, i + 1)
                nc.vector.tensor_tensor(wk_lo[:, s, :, :], wk_staged[i % 2], wk_hi[:, s, :, :], ALU.subtract)
                low(wv_lo[:, s, :, :], wv_staged[i % 2], wv_hi[:, s, :, :], w_low)

            def low_ip(k):
                dve.wait_ge(ip_high, k + 1)
                low(ip_lo[:, :, :], ip_staged, ip_hi[:, :, :], ip_low)

            def rest_of(t, s, n, bank, hi, rest_at, first=False):
                dve.wait_ge(k_hi, t + 1)
                if not first:
                    dve.wait_ge(k_lo, t - 1)
                nc.vector.tensor_tensor(keys(rest[:, rest_at, 0:n], s), keys(k_ps[bank][:, 0:n], s), hi,
                                        ALU.subtract).then_inc(k_rest, 1)

            def pad(v, bank, buf, n):
                dve.wait_ge(v_proj, v + 1)
                src = v_ps[bank][0:n, 0:C].rearrange("p (g j d) -> p g j d", g=G, j=4)
                nc.vector.tensor_copy(v_pad[0:n, buf, 0:G:2, :, 0:HD], src[:, 0:G:2, :, :])
                nc.vector.tensor_copy(v_pad[0:n, buf, 1:G:2, :, HD:2 * HD], src[:, 1:G:2, :, :])
                nc.vector.tensor_copy(v_pad[0:n, buf, G - 1, :, HD:2 * HD], src[:, G - 1, :, :]).then_inc(v_cast, 1)

            def small(i):
                s = GROUPS[i]
                for c in range(NC):
                    t = NC * i + c
                    rest_of(t, s, SMALL, t % KB, small_view(0, s, c), t % 2, t < 2)
                for h in range(2):
                    pad(2 * i + h, 2 * i + h, 2 * i + h, P)

            dve.wait_ge(v_zero, 1)
            dve.wait_ge(small_high, 1)
            low(small_lo, small_staged, small_hi, small_low)
            low_weights(0)
            low_weights(1)
            small(0)
            low_weights(2)
            small(1)
            low_ip(0)
            low_weights(3)

            def low_projections():
                wq_hi, wq_lo, wo_hi, wo_lo = (const[n] for n in ("wq_hi", "wq_lo", "wo_hi", "wo_lo"))
                dve.wait_ge(proj_high, 1)
                low(wq_lo[:, :, :], wq_staged, wq_hi[:, :, :], proj_low)
                low(wo_lo[:, :, :], wo_staged, wo_hi[:, :, :], proj_low)
                dve.wait_ge(proj_low, 2)
                nc.vector.tensor_scalar_mul(wo_hi[:, 2, :], wo_hi[:, 2, :], halves[:, 0:1]).then_inc(proj_low, 1)
                nc.vector.tensor_scalar_mul(wo_lo[:, 2, :], wo_lo[:, 2, :], halves[:, 1:2]).then_inc(proj_low, 1)
                dve.wait_ge(proj_low, 4)
                nc.vector.tensor_tensor(wo_lo[:, 2, :], wo_lo[:, 2, :], wo_hi[:, 2, :], ALU.add).then_inc(proj_low, 1)

            def step(k, r, last):
                dve.wait_ge(txt_high, k + 1)
                low(chunks(txt_lo[:, :]), txt_staged, chunks(txt_hi[:, :]), txt_low)

                def half(k_tiles, v_tiles, between=None):
                    for x in k_tiles:
                        c, b0, nb, s = KTILES[x]
                        rest_of(SKT + NKT * k + x, s, nb * SEG[s][1], x % KB,
                                block_view(r, 0, c, b0, nb, s), (NKT * r + x) % 2)
                    if between:
                        between()
                    for x in v_tiles:
                        dve.wait_ge(v_out[x % NV], 16 * (2 * k + x // NV + 1))
                        pad(SVT + NVT * k + x, x % 4, x % NV, VTILES[x][2])

                half(range(IKT), range(IVT))
                half(range(IKT, NKT), range(IVT, NVT), low_projections if last else lambda: low_ip(k + 1))

            run_blocks(dve, step)

        @block.gpsimd
        def _(pool):
            def low(t, s, n, mid, lo, rest_at):
                pool.wait_ge(k_mid, t + 1)
                nc.gpsimd.tensor_tensor(lo, keys(rest[:, rest_at, 0:n], s), mid, ALU.subtract).then_inc(k_lo, 1)

            for i, s in enumerate(GROUPS[:2]):
                for c in range(NC):
                    t = NC * i + c
                    low(t, s, SMALL, small_view(1, s, c), small_view(2, s, c), t % 2)

            def step(k, r, last):
                for x, (c, b0, nb, s) in enumerate(KTILES):
                    low(SKT + NKT * k + x, s, nb * SEG[s][1], block_view(r, 1, c, b0, nb, s),
                        block_view(r, 2, c, b0, nb, s), (NKT * r + x) % 2)

            run_blocks(pool, step)


def attention_phase(nc, x_t, k_shift, const, k_parts, v_rows, out_t):
    ctx = ExitStack()
    with ctx:
        def sb(name, shape, dt):
            return ctx.enter_context(nc.sbuf_tensor(name, shape, dt))

        def ps(name, shape, dt):
            return ctx.enter_context(nc.psum_tensor(name, shape, dt))

        def sem(name):
            return ctx.enter_context(nc.semaphore(name))

        def ring(name):
            return [sem(f"{name}{i}") for i in range(R)]

        R = 3
        LAST = B - 1 + LATEST

        wq_hi, wq_lo, wo_hi, wo_lo = (const[n] for n in ("wq_hi", "wq_lo", "wo_hi", "wo_lo"))
        bias_sb, den_sb, bcast_sb, ident = (const[n] for n in ("bias", "e_den", "e_bcast", "ident"))
        x_sb = sb("x_sb", [P, NC, S], F32)
        x_hi = sb("x_hi", [P, NC, S], F32R)
        x_lo = sb("x_lo", [P, NC - 1, S], F32R)
        xres = sb("xres", [P, R, NC, S], F32)
        q_part = sb("q_part", [P, R, PARTS, NC, S], BF16)
        q_rest = sb("q_rest", [P, NC, S], F32)
        q_stack = sb("q_stack", [NROW + SHIFT, R, SLOTS, S], BF16)
        k_stack = sb("k_stack", [NROW + SHIFT, R, SLOTS, NKEY], BF16)
        v_sb = sb("v_sb", [NKEY, R, HEADS, 32], F32)
        m_sb = sb("m_sb", [P, R, 2, NSEG, SLOTS], F32)
        m_rest = sb("m_rest", [P, 2, NSEG * SLOTS], F32)
        m_part = sb("m_part", [P, PARTS, 2, NSEG * SLOTS], BF16)
        m_t = sb("m_t", [NSEG * SLOTS, PARTS, S], BF16)
        p_sb = sb("p_sb", [NKEY, R, HEADS, S], F32)
        den = sb("den", [P, S], F32)
        inv = sb("inv", [P, S], F32)
        inv_rest = sb("inv_rest", [P, S], F32)
        inv_part = sb("inv_part", [P, PARTS, S], BF16)
        inv_stack = sb("inv_stack", [NROW, R, 4, S], BF16)
        t_raw = sb("t_raw", [P, S], F32)
        att_hi = sb("att_hi", [P, R, NC, S], F32R)
        att_lo = sb("att_lo", [P, R, NC, S], F32R)

        a_ps = ps("a_ps", [P, 2, 512], F32)
        b_ps = ps("b_ps", [P, 2, S], F32)
        r_ps = ps("r_ps", [P, 2, S], F32)
        q_ps = ps("q_ps", [P, 512], F32)
        d_ps = ps("d_ps", [P, 512], F32)
        t_ps = ps("t_ps", [P, 512], F32)
        o_ps = ps("o_ps", [P, 512], F32)
        mt_ps = q_ps[0:NSEG * SLOTS, 0:PARTS * S // 2].bitcast(BF16).rearrange("p (a q) -> p a q", a=PARTS)

        shift_in = sem("shift_in")
        zeroed = sem("zeroed")
        x_in = sem("x_in")
        k_in, v_in, xres_in = ring("k_in"), ring("v_in"), ring("xres_in")
        x_high = sem("x_high")
        x_low = sem("x_low")
        q_in, m_in = ring("q_in"), ring("m_in")
        stored = ring("stored")
        q_done = sem("q_done")
        q_hi, q_mid = sem("q_hi"), sem("q_mid")
        q_left = sem("q_left")
        q_lo = sem("q_lo")
        a_done = sem("a_done")
        max_done = sem("max_done")
        m_hi, m_mid = sem("m_hi"), sem("m_mid")
        m_left, m_lo = sem("m_left"), sem("m_lo")
        mt_done = sem("mt_done")
        mt_copied = sem("mt_copied")
        b_done = sem("b_done")
        exp_done = sem("exp_done")
        d_done = sem("d_done")
        d_copied = sem("d_copied")
        recip_done = sem("recip_done")
        i_hi, i_mid = sem("i_hi"), sem("i_mid")
        i_left, i_lo = sem("i_left"), sem("i_lo")
        hi_stacked = sem("hi_stacked")
        i_stacked = sem("i_stacked")
        r_done = sem("r_done")
        p_done = sem("p_done")
        v_done = sem("v_done")
        t_copied = sem("t_copied")
        t_low = sem("t_low")
        o_done = sem("o_done")
        out_done = sem("out_done")

        block = ctx.enter_context(nc.Block())

        class Step:

            def __init__(self, g, r):
                self.g, self.r, self.known = g, r, isinstance(g, int)

            def live(self, k):
                return not self.known or 0 <= 3 * self.g + self.r - k < B

            def since(self, k, n):
                return not self.known or 3 * self.g + self.r - k >= n

            def batch(self, k):
                return 3 * self.g + (self.r - k)

            def buf(self, k):
                return (self.r - k) % R

            def turn(self, k):
                return self.g + (self.r - k) // R

        FIRST = 2
        LOOPED = B // R

        def run(eng, iteration):
            for g in range(FIRST):
                for r in range(R):
                    iteration(Step(g, r))
            with eng.Fori(FIRST, LOOPED) as g:
                for r in range(R):
                    iteration(Step(g, r))
            for i in range(LOOPED * R, LAST + 1):
                iteration(Step(i // R, i % R))

        A_BANKS = [((0, 0), (0, 1)), ((0, 2), (0, 3)), ((1, 0), (1, 1)), ((1, 2), (1, 3)), ((0, 4), (1, 4))]

        def rows_of(c):
            return P if c < 2 else C - 2 * P

        @block.sync
        def _(sp):
            def load_x(dst, b, done):
                sp.dma_start(dst[:, 0:2, :], x_t[bass.ds(b, 1), 0:2 * P, :].rearrange("o (c p) q -> p (o c) q", p=P)).then_inc(done, 16)
                sp.dma_start(dst[0:C - 2 * P, 2, :], x_t[bass.ds(b, 1), 2 * P:C, :].rearrange("o p q -> (o p) q")).then_inc(done, 16)

            load_x(x_sb, 0, x_in)
            for i in range(R):
                sp.dma_start(k_stack[NROW:, i, :, :], k_shift).then_inc(shift_in, 16)

            def iteration(s):
                if s.live(-1):
                    sp.wait_ge(x_low, 2 * s.batch(-1))
                    load_x(x_sb, s.batch(-1), x_in)
                if s.live(0):
                    b, i = s.batch(0), s.buf(0)
                    if s.since(0, R):
                        sp.wait_ge(b_done, UNITS * b - UNITS * R + UNITS)
                    row = 0
                    for n in (3, 2, 1):
                        sp.dma_start(k_stack[row:row + n * HD, i, :, :].rearrange("r s n -> r (s n)"),
                                     k_parts[bass.ds(b, 1), 0:n, :, :, :].rearrange("o a (d h) c n -> (o a d) (h c n)", d=HD)).then_inc(k_in[i], 16)
                        row += n * HD
                if s.live(0):
                    b, i = s.batch(0), s.buf(0)
                    sp.wait_ge(q_lo, 3 * b + 3)
                    for row, part in enumerate(QPART):
                        sp.dma_start(q_stack[row * HD:(row + 1) * HD, i, :, :], q_part[:, i, part, :, :]).then_inc(q_in[i], 16)
                if s.live(1):
                    b, i = s.batch(1), s.buf(1)
                    if s.since(1, R):
                        sp.wait_ge(v_done, UNITS * b - UNITS * R + UNITS)
                    for (at, n), rows in zip(SEG, v_rows):
                        sp.dma_start(v_sb[at:at + n, i, :, :].rearrange("p h d -> p (h d)"), rows[bass.ds(n * b, n), :]).then_inc(v_in[i], 16)
                if s.live(3):
                    b, i = s.batch(3), s.buf(3)
                    if s.since(3, R):
                        sp.wait_ge(stored[i], 32 * s.turn(3))
                    load_x(xres[:, i, :, :], b, xres_in[i])
                if s.live(1):
                    b, i = s.batch(1), s.buf(1)
                    sp.wait_ge(mt_copied, b + 1)
                    for part in range(PARTS):
                        row = NROW + NSEG * part
                        sp.dma_start(q_stack[row:row + NSEG, i, :, :], m_t[:, part, :]).then_inc(m_in[i], 16)
                if s.live(LATEST):
                    b, i = s.batch(LATEST), s.buf(LATEST)
                    sp.wait_ge(out_done, 3 * b + 3)
                    sp.dma_start(out_t[bass.ds(b, 1), 0:2 * P, :].rearrange("o (c p) q -> p (o c) q", p=P), xres[:, i, 0:2, :]).then_inc(stored[i], 16)
                    sp.dma_start(out_t[bass.ds(b, 1), 2 * P:C, :].rearrange("o p q -> (o p) q"), xres[0:C - 2 * P, i, 2, :]).then_inc(stored[i], 16)

            run(sp, iteration)
            for i in range(R):
                sp.wait_ge(stored[i], 32 * len(range(i, B, R)))

        @block.tensor
        def _(pe):
            def project_q(s, age, x):
                c, k = divmod(x, NC)
                b, i = s.batch(age), s.buf(age)
                if x == 0:
                    pe.wait_ge(x_low, 2 * b + 1)
                    if s.since(age, 2):
                        pe.wait_ge(mt_copied, b - 1)
                elif k == 0:
                    pe.wait_ge(q_hi, 3 * b + c)
                if x == NC - 1:
                    pe.wait_ge(x_low, 2 * b + 2)
                col = slice(c * P, (c + 1) * P)
                nc.tensor.matmul(q_ps[:, 0:S], wq_hi[:, k, col], x_hi[:, k, :], start=(k == 0), stop=False)
                if k < NC - 1:
                    nc.tensor.matmul(q_ps[:, 0:S], wq_hi[:, k, col], x_lo[:, k, :], start=False, stop=False)
                n = rows_of(k)
                last = nc.tensor.matmul(q_ps[:, 0:S], wq_lo[0:n, k, col], x_hi[0:n, k, :], start=False, stop=(k == NC - 1))
                if k == NC - 1:
                    last.then_inc(q_done, 1)

            def scores_for_max(s, k, a):
                b, i = s.batch(k), s.buf(k)
                if a == 0:
                    pe.wait_ge(q_in[i], 16 * len(QPART) * (s.turn(k) + 1))
                    pe.wait_ge(k_in[i], 48 * (s.turn(k) + 1))
                if a > 0 or s.since(k, 1):
                    pe.wait_ge(max_done, 5 * b + a)
                for bank, (half, g) in enumerate(A_BANKS[a]):
                    for j in range(4):
                        at = slot(4 * g + j)
                        last = nc.tensor.matmul(a_ps[:, bank, j * NKEY:(j + 1) * NKEY],
                                                q_stack[0:NROW, i, at, half * P:(half + 1) * P],
                                                k_stack[0:NROW, i, at, :], start=True, stop=True)
                last.then_inc(a_done, 1)

            def transpose_max(s, age):
                b = s.batch(age)
                pe.wait_ge(m_lo, b + 1)
                if s.live(age - 1):
                    pe.wait_ge(q_hi, 3 * b + 6)
                for part in range(PARTS):
                    for half in range(2):
                        last = nc.tensor.transpose(mt_ps[:, part, half * P:(half + 1) * P], m_part[:, part, half, :], ident[:, :])
                last.then_inc(mt_done, 1)

            def scores(s, k, u):
                b, i = s.batch(k), s.buf(k)
                if u == 0:
                    pe.wait_ge(shift_in, 16 * R)
                    pe.wait_ge(m_in[i], 48 * (s.turn(k) + 1))
                if u > 0 or s.since(k, 1):
                    pe.wait_ge(exp_done, UNITS * b + u)
                for h in range(2):
                    at = slot(2 * u + h)
                    last = nc.tensor.matmul(b_ps[0:NKEY, h, :], k_stack[:, i, at, :], q_stack[:, i, at, :], start=True, stop=True)
                last.then_inc(b_done, 1)

            def reciprocals(s, k, u):
                b, i = s.batch(k), s.buf(k)
                if u == 0:
                    pe.wait_ge(hi_stacked, b + 1)
                    pe.wait_ge(i_stacked, b + 1)
                if u > 0 or s.since(k, 1):
                    pe.wait_ge(p_done, UNITS * b + u)
                for h in range(2):
                    g, j = divmod(2 * u + h, 4)
                    last = nc.tensor.matmul(r_ps[0:NKEY, h, :], bcast_sb[:, g, :], inv_stack[:, i, j, :], start=True, stop=True)
                last.then_inc(r_done, 1)

            def denominators(s, k, u):
                b, i = s.batch(k), s.buf(k)
                pe.wait_ge(exp_done, UNITS * b + u + 1)
                if u == 0 and s.since(k, 1):
                    pe.wait_ge(d_copied, b)
                for h in range(2):
                    g, j = divmod(2 * u + h, 4)
                    last = nc.tensor.matmul(d_ps[32 * j:32 * j + 32, 0:S], den_sb[:, g, :], p_sb[:, i, 2 * u + h, :],
                                            start=(g == 0), stop=(g == G - 1), tile_position=(0, 32 * j), skip_group_check=True)
                if u == UNITS - 1:
                    last.then_inc(d_done, 1)

            def attend(s, k, u):
                b, i = s.batch(k), s.buf(k)
                pe.wait_ge(p_done, UNITS * b + u + 1)
                if u == 0:
                    pe.wait_ge(v_in[i], 64 * (s.turn(k) + 1))
                if u in (0, 4, 8) and (u > 0 or s.since(k, 1)):
                    pe.wait_ge(t_copied, 3 * b + u // 4)
                for h in range(2):
                    g, j = divmod(2 * u + h, 4)
                    last = nc.tensor.matmul(t_ps[32 * j:32 * j + 32, 0:S], v_sb[:, i, 2 * u + h, :], p_sb[:, i, 2 * u + h, :],
                                            start=(g % 2 == 0), stop=(g % 2 == 1 or g == G - 1), tile_position=(0, 32 * j), skip_group_check=True)
                last.then_inc(v_done, 1)

            def project_out(s, age, x):
                c, k = divmod(x, NC)
                b, i = s.batch(age), s.buf(age)
                if c == 0:
                    pe.wait_ge(t_low, 3 * b + k + 1)
                if k == 0 and (c > 0 or s.since(age, 1)):
                    pe.wait_ge(out_done, 3 * b + c)
                m = rows_of(c)
                col = slice(c * P, c * P + m)
                nc.tensor.matmul(o_ps[0:m, 0:S], wo_lo[:, k, col], att_hi[:, i, k, :], start=(k == 0), stop=False)
                if k < NC - 1:
                    nc.tensor.matmul(o_ps[0:m, 0:S], wo_hi[:, k, col], att_hi[:, i, k, :], start=False, stop=False)
                last = nc.tensor.matmul(o_ps[0:m, 0:S], wo_hi[:, k, col], att_lo[:, i, k, :], start=False, stop=(k == NC - 1))
                if k == NC - 1:
                    last.then_inc(o_done, 1)

            def iteration(s):
                for w in range(UNITS):
                    for k, u in due(pairs(SCORES), w):
                        if s.live(k):
                            scores(s, k, u)
                    for k, u in due(pairs(NORMS), w):
                        if s.live(k):
                            reciprocals(s, k, u)
                    for k, x in due(Q_AT, w):
                        if s.live(k):
                            project_q(s, k, x)
                    for k, a in due(MAX_AT, w):
                        if s.live(k):
                            scores_for_max(s, k, a)
                    for k, u in due(pairs(ATTENDS), w):
                        if s.live(k):
                            attend(s, k, u)
                    for k, x in due(O_AT, w):
                        if s.live(k):
                            project_out(s, k, x)
                    for k, _ in due((MT_AT,), w):
                        if s.live(k):
                            transpose_max(s, k)
                    for k, u in due(pairs(DENS), w):
                        if s.live(k):
                            denominators(s, k, u)

            run(pe, iteration)

        @block.scalar
        def _(act):
            def high_x(b):
                act.wait_ge(x_in, 32 * b + 32)
                nc.scalar.activation(x_hi[:, 0:2, :], x_sb[:, 0:2, :], ACT.Copy)
                nc.scalar.activation(x_hi[0:P // 2, 2, :], x_sb[0:P // 2, 2, :], ACT.Copy).then_inc(x_high, 1)

            def high_q(s, k, c):
                b, i = s.batch(k), s.buf(k)
                act.wait_ge(q_done, 3 * b + c + 1)
                if c == 0 and s.since(k, R):
                    act.wait_ge(q_in[i], 16 * len(QPART) * s.turn(k))
                nc.scalar.activation(q_part[:, i, 0, c, :], q_ps[:, 0:S], ACT.Copy)
                if s.since(k, 1):
                    act.wait_ge(q_lo, 3 * b - 3 + c + 1)
                nc.scalar.activation(q_rest[:, c, :], q_ps[:, 0:S], ACT.Copy).then_inc(q_hi, 1)

            def mid_q(s, k, c):
                b, i = s.batch(k), s.buf(k)
                act.wait_ge(q_left, 3 * b + c + 1)
                nc.scalar.activation(q_part[:, i, 1, c, :], q_rest[:, c, :], ACT.Copy).then_inc(q_mid, 1)

            def exponentials(s, k, u):
                b, i = s.batch(k), s.buf(k)
                act.wait_ge(b_done, UNITS * b + u + 1)
                if u == 0 and s.since(k, R):
                    act.wait_ge(v_done, UNITS * b - UNITS * R + UNITS)
                nc.scalar.activation(p_sb[:, i, 2 * u:2 * u + 2, :], b_ps[0:NKEY, :, :], ACT.Exp, scale=SCALE).then_inc(exp_done, 1)

            def high_max(s, k):
                b, i = s.batch(k), s.buf(k)
                act.wait_ge(max_done, 5 * b + 5)
                if s.since(k, 1):
                    act.wait_ge(mt_done, b)
                nc.scalar.activation(m_part[:, 0, :, :], m_sb[:, i, :, :, :].rearrange("p a s h -> p a (s h)"), ACT.Copy).then_inc(m_hi, 1)

            def mid_max(s, k):
                b = s.batch(k)
                act.wait_ge(m_left, b + 1)
                nc.scalar.activation(m_part[:, 1, :, :], m_rest[:, :, :], ACT.Copy).then_inc(m_mid, 1)

            def copy_max(s, k):
                b = s.batch(k)
                act.wait_ge(mt_done, b + 1)
                if s.since(k, 1):
                    act.wait_ge(m_in[s.buf(k + 1)], 48 * (s.turn(k + 1) + 1))
                nc.scalar.activation(m_t[:, :, :], mt_ps, ACT.Copy).then_inc(mt_copied, 1)

            def copy_den(s, k):
                b = s.batch(k)
                act.wait_ge(d_done, b + 1)
                if s.since(k, 1):
                    act.wait_ge(recip_done, b)
                nc.scalar.activation(den[:, :], d_ps[:, 0:S], ACT.Copy).then_inc(d_copied, 1)

            def high_inv(s, k):
                b = s.batch(k)
                act.wait_ge(recip_done, b + 1)
                if s.since(k, 1):
                    act.wait_ge(hi_stacked, b)
                    act.wait_ge(i_left, b)
                nc.scalar.activation(inv_part[:, 0, :], inv[:, :], ACT.Copy).then_inc(i_hi, 1)

            def mid_inv(s, k):
                b = s.batch(k)
                act.wait_ge(i_left, b + 1)
                if s.since(k, 1):
                    act.wait_ge(i_stacked, b)
                nc.scalar.activation(inv_part[:, 1, :], inv_rest[:, :], ACT.Copy).then_inc(i_mid, 1)

            def copy_attention(s, k, c):
                b, i = s.batch(k), s.buf(k)
                act.wait_ge(v_done, UNITS * b + (4, 8, 10)[c])
                if c == 0 and s.since(k, R):
                    act.wait_ge(o_done, 3 * b - 3 * R + 3)
                if c > 0 or s.since(k, 1):
                    act.wait_ge(t_low, 3 * b + c)
                nc.scalar.activation(att_hi[:, i, c, :], t_ps[:, 0:S], ACT.Copy)
                nc.scalar.activation(t_raw[:, :], t_ps[:, 0:S], ACT.Copy).then_inc(t_copied, 1)

            def iteration(s):
                for w in range(UNITS):
                    for k, _ in due((DEN_COPY,), w):
                        if s.live(k):
                            copy_den(s, k)
                    for k, u in due(pairs(SCORES), w):
                        if s.live(k):
                            exponentials(s, k, u)
                    for k, c in due(Q_HIGH, w):
                        if s.live(k):
                            high_q(s, k, c)
                    for k, _ in due((INV_HIGH,), w):
                        if s.live(k):
                            high_inv(s, k)
                    for k, _ in due((INV_MID,), w):
                        if s.live(k):
                            mid_inv(s, k)
                    for k, c in due(T_COPY, w):
                        if s.live(k):
                            copy_attention(s, k, c)
                    for k, _ in due((MAX_HIGH,), w):
                        if s.live(k):
                            high_max(s, k)
                    for k, c in due(Q_MID, w):
                        if s.live(k):
                            mid_q(s, k, c)
                    for k, _ in due((MAX_MID,), w):
                        if s.live(k):
                            mid_max(s, k)
                    for k, _ in due((X_AT,), w):
                        if s.live(k):
                            act.wait_ge(q_done, 3 * s.batch(k))
                            high_x(s.batch(k))
                    for k, _ in due((MT_AT,), w):
                        if s.live(k):
                            copy_max(s, k)

            high_x(0)
            run(act, iteration)

        @block.vector
        def _(dve):
            for i in range(R):
                nc.vector.memset(m_sb[:, i, :, :, :], 0.0).then_inc(zeroed, 1)

            def maxima(s, k, a):
                b, i = s.batch(k), s.buf(k)
                dve.wait_ge(a_done, 5 * b + a + 1)
                if a == 0 and s.since(k, R):
                    dve.wait_ge(m_left, b - R + 1)
                src = a_ps[:, :, 0:4 * NKEY].rearrange("p a (j n) -> p a j n", j=4)
                (h0, g0), (h1, g1) = A_BANKS[a]

                def dst(s0, s1):
                    m = m_sb[:, i, :, s0:s1, :].rearrange("p q s (e j c) -> p q e j c s", e=2, j=4)
                    if h0 == h1:
                        return m[:, h0, :, :, g0 // 2, :]
                    return m[:, :, 0, :, g0 // 2, :]

                for first, count in ((0, 1), (3, 1)):
                    at, n = SEG[first]
                    nc.vector.tensor_reduce(dst(first, first + 1), src[:, :, :, at:at + n], AX.X, ALU.max)
                at, n = SEG[1]
                small = src[:, :, :, at:at + 2 * n].rearrange("p a j (s n) -> p a j s n", s=2)
                nc.vector.tensor_reduce(dst(1, 3), small, AX.X, ALU.max).then_inc(max_done, 1)

            def invert(s, k):
                b = s.batch(k)
                dve.wait_ge(d_copied, b + 1)
                if s.since(k, 1):
                    dve.wait_ge(i_left, b)
                nc.vector.reciprocal(inv[:, :], den[:, :]).then_inc(recip_done, 1)

            def stack_high_inv(s, k):
                b, i = s.batch(k), s.buf(k)
                dve.wait_ge(i_hi, b + 1)
                if s.since(k, R):
                    dve.wait_ge(r_done, UNITS * b - UNITS * R + UNITS)
                for j in range(4):
                    last = nc.vector.tensor_copy(inv_stack[0:32, i, j, :], inv_part[32 * j:32 * j + 32, 0, :])
                last.then_inc(hi_stacked, 1)

            def stack_inv(s, k):
                b, i = s.batch(k), s.buf(k)
                dve.wait_ge(i_lo, b + 1)
                if s.since(k, R):
                    dve.wait_ge(r_done, UNITS * b - UNITS * R + UNITS)
                for part in range(1, PARTS):
                    for j in range(4):
                        last = nc.vector.tensor_copy(inv_stack[32 * part:32 * part + 32, i, j, :], inv_part[32 * j:32 * j + 32, part, :])
                last.then_inc(i_stacked, 1)

            def normalise(s, k, u):
                b, i = s.batch(k), s.buf(k)
                dve.wait_ge(r_done, UNITS * b + u + 1)
                both = p_sb[:, i, 2 * u:2 * u + 2, :]
                nc.vector.tensor_tensor(both, r_ps[0:NKEY, :, :], both, ALU.mult).then_inc(p_done, 1)

            def finish(s, k, c):
                b, i = s.batch(k), s.buf(k)
                dve.wait_ge(o_done, 3 * b + c + 1)
                if c == 0:
                    dve.wait_ge(xres_in[i], 32 * (s.turn(k) + 1))
                m = rows_of(c)
                nc.vector.scalar_tensor_tensor(out=xres[0:m, i, c, :], in0=o_ps[0:m, 0:S], scalar=bias_sb[0:m, c:c + 1],
                                               in1=xres[0:m, i, c, :], op0=ALU.add, op1=ALU.add).then_inc(out_done, 1)

            def iteration(s):
                for w in range(UNITS):
                    for k, _ in due((INVERT,), w):
                        if s.live(k):
                            invert(s, k)
                    for k, u in due(pairs(NORMS), w):
                        if s.live(k):
                            normalise(s, k, u)
                    for k, _ in due((INV_MID,), w):
                        if s.live(k):
                            stack_high_inv(s, k)
                    for k, a in due(MAX_AT, w):
                        if s.live(k):
                            maxima(s, k, a)
                    for k, c in due(O_AT[2::3], w):
                        if s.live(k):
                            finish(s, k, c)
                    for k, _ in due((INV_STACK,), w):
                        if s.live(k):
                            stack_inv(s, k)

            dve.wait_ge(zeroed, R)
            run(dve, iteration)

        @block.gpsimd
        def _(pool):
            def left_q(s, k, c):
                b, i = s.batch(k), s.buf(k)
                pool.wait_ge(q_hi, 3 * b + c + 1)
                nc.gpsimd.tensor_tensor(q_rest[:, c, :], q_rest[:, c, :], q_part[:, i, 0, c, :], ALU.subtract).then_inc(q_left, 1)

            def low_q(s, k, c):
                b, i = s.batch(k), s.buf(k)
                pool.wait_ge(q_mid, 3 * b + c + 1)
                nc.gpsimd.tensor_tensor(q_part[:, i, 2, c, :], q_rest[:, c, :], q_part[:, i, 1, c, :], ALU.subtract).then_inc(q_lo, 1)

            def left_max(s, k):
                b, i = s.batch(k), s.buf(k)
                pool.wait_ge(m_hi, b + 1)
                if s.since(k, 1):
                    pool.wait_ge(m_lo, b)
                nc.gpsimd.tensor_tensor(m_rest[:, :, :], m_sb[:, i, :, :, :].rearrange("p a s h -> p a (s h)"),
                                        m_part[:, 0, :, :], ALU.subtract).then_inc(m_left, 1)

            def low_max(s, k):
                b = s.batch(k)
                pool.wait_ge(m_mid, b + 1)
                nc.gpsimd.tensor_tensor(m_part[:, 2, :, :], m_rest[:, :, :], m_part[:, 1, :, :], ALU.subtract).then_inc(m_lo, 1)

            def left_inv(s, k):
                b = s.batch(k)
                pool.wait_ge(i_hi, b + 1)
                if s.since(k, 1):
                    pool.wait_ge(i_lo, b)
                nc.gpsimd.tensor_tensor(inv_rest[:, :], inv[:, :], inv_part[:, 0, :], ALU.subtract).then_inc(i_left, 1)

            def low_inv(s, k):
                b = s.batch(k)
                pool.wait_ge(i_mid, b + 1)
                nc.gpsimd.tensor_tensor(inv_part[:, 2, :], inv_rest[:, :], inv_part[:, 1, :], ALU.subtract).then_inc(i_lo, 1)

            def low_x(b):
                pool.wait_ge(x_high, b + 1)
                nc.gpsimd.tensor_tensor(x_lo[:, :, :], x_sb[:, 0:2, :], x_hi[:, 0:2, :], ALU.subtract).then_inc(x_low, 1)
                pool.wait_ge(x_low, 2 * b + 1)
                nc.gpsimd.tensor_tensor(x_hi[P // 2:P, 2, :], x_sb[0:P // 2, 2, :], x_hi[0:P // 2, 2, :], ALU.subtract).then_inc(x_low, 1)
                pool.wait_ge(x_low, 2 * b + 2)

            def low_attention(s, k, c):
                b, i = s.batch(k), s.buf(k)
                pool.wait_ge(t_copied, 3 * b + c + 1)
                nc.gpsimd.tensor_tensor(att_lo[:, i, c, :], t_raw[:, :], att_hi[:, i, c, :], ALU.subtract).then_inc(t_low, 1)

            def iteration(s):
                for w in range(UNITS):
                    for k, c in due(Q_LEFT, w):
                        if s.live(k):
                            left_q(s, k, c)
                    for k, c in due(T_COPY, w):
                        if s.live(k):
                            low_attention(s, k, c)
                    for k, c in due(Q_MID, w):
                        if s.live(k):
                            low_q(s, k, c)
                    for k, _ in due((INV_HIGH,), w):
                        if s.live(k):
                            left_inv(s, k)
                    for k, _ in due((MAX_HIGH,), w):
                        if s.live(k):
                            left_max(s, k)
                    for k, _ in due((INV_LOW,), w):
                        if s.live(k):
                            low_inv(s, k)
                    for k, _ in due((MAX_MID,), w):
                        if s.live(k):
                            low_max(s, k)
                    for k, _ in due((X_AT,), w):
                        if s.live(k):
                            low_x(s.batch(k))

            low_x(0)
            run(pool, iteration)


def cross_attention(nc, a, out_t):
    k_parts = nc.dram_tensor("k_parts", [B, PARTS, P, NC, NKEY], BF16, kind="Internal").ap()
    v_rows = [nc.dram_tensor(f"v_rows{s}", [B * n, HEADS * 32], F32, kind="Internal").ap() for s, (_, n) in enumerate(SEG)]
    ctx = ExitStack()
    with ctx:
        const = constant_tensors(nc, ctx)
        context_phase(nc, a["ctx_txt"], a["ctx_ip"], a["ctx_small"], [a[f"wk{s}"] for s in range(NSEG)],
                      [a[f"wv{s}"] for s in range(NSEG)], a, const, k_parts, v_rows)
        attention_phase(nc, a["x_t"], a["k_shift"], const, k_parts, v_rows, out_t)


def constants():
    import numpy as np
    bf = np.dtype("bfloat16")
    k_shift = np.zeros((PARTS, NSEG, SLOTS, NKEY), bf)
    e_den = np.zeros((NKEY, G, 32), np.float32)
    e_den[:, 0, 4 * G:] = 1.0
    e_bcast = np.zeros((PARTS, 32, G, NKEY), bf)
    for s, (at, n) in enumerate(SEG):
        k_shift[:, s, :, at:at + n] = -1.0
        for g in range(G):
            e_den[at:at + n, g, 4 * g + s] = 1.0
            e_bcast[:, 4 * g + s, g, at:at + n] = 1.0
    wo_rows = np.zeros((4, 2, HD, 2), np.float32)
    wo_rows[:, 0, :, 0] = wo_rows[:, 1, :, 1] = 1.0
    return {
        "wo_rows": wo_rows.reshape(P, 2), "k_shift": k_shift.reshape(SHIFT, SLOTS, NKEY), "e_den": e_den,
        "e_bcast": e_bcast.reshape(NROW, G, NKEY), "ident": np.eye(P, dtype=bf),
    }


def kernel(**inputs):
    import numpy as np
    import concourse.bacc as bacc
    from concourse.bass_utils import run_bass_kernel_spmd

    w = {n[len("L0_xattn_to_"):]: np.asarray(v) for n, v in inputs.items() if n.startswith("L0_")}
    x, context = np.asarray(inputs["x"]), np.asarray(inputs["ctx_2048"])

    def head_columns(m):
        full = np.zeros((m.shape[0], NC * 8, HD), m.dtype)
        full[:, :HEADS] = m.reshape(-1, HEADS, HD)
        return np.ascontiguousarray(full.reshape(-1, NC, 8, HD).transpose(0, 1, 3, 2)).reshape(-1, NC * P)

    def tokens(first, n, batches):
        part = context[:, first:first + n].reshape(B // batches, batches * n, CTX)
        return part.transpose(0, 2, 1)

    wo = np.zeros((2 * NC, 4, HD, C), w["out_w"].dtype)
    wo[:G] = w["out_w"].reshape(G, 4, HD, C)
    wo[G] = wo[G - 1]
    wo = wo.reshape(NC, 2, 4, HD, C).transpose(0, 2, 1, 3, 4)
    arrays = {
        "x_t": x.transpose(0, 2, 1),
        "ctx_txt": tokens(*SEG[0], PB), "ctx_ip": tokens(*SEG[3], PB),
        "ctx_small": np.concatenate([tokens(*SEG[1], B)[0], tokens(*SEG[2], B)[0]], axis=1),
        "wq": head_columns(w["q_w"]), "wo": wo.reshape(NC, P, C), "bias": w["out_b"],
    }
    for s, name in enumerate(("", "_object", "_others", "_ip")):
        arrays[f"wk{s}"] = head_columns(w[f"k{name}_w"])
        arrays[f"wv{s}"] = w[f"v{name}_w"]
    arrays.update(constants())
    arrays = {n: np.ascontiguousarray(v) for n, v in arrays.items()}

    nc = bacc.Bacc("TRN2", target_bir_lowering=False, num_devices=1)
    aps = {n: nc.dram_tensor(f"in_{n}", v.shape, mybir.dt.from_np(v.dtype), kind="ExternalInput").ap() for n, v in arrays.items()}
    out = nc.dram_tensor("out_t", (B, C, S), F32, kind="ExternalOutput").ap()
    cross_attention(nc, aps, out)
    r = run_bass_kernel_spmd(nc, [{f"in_{n}": v for n, v in arrays.items()}], core_ids=[0])
    return r.results[0]["out_t"].transpose(0, 2, 1)
```
